# Optimizing a Trainium2 kernel written in Bass

```python
import numpy as np
import jax
import jax.numpy as jnp

def _softmax(x, axis=-1):
    return jax.nn.softmax(x, axis=axis)

def _gelu(x):
    return jax.nn.gelu(x, approximate=True)

def _silu(x):
    return jax.nn.silu(x)

def _sigmoid(x):
    return jax.nn.sigmoid(x)

def _layernorm(x, axis=-1, eps=1e-05):
    m = jnp.mean(x, axis=axis, keepdims=True)
    v = jnp.var(x, axis=axis, keepdims=True)
    return (x - m) / jnp.sqrt(v + eps)

def _scatter_add(tgt, idx, src, axis=0):
    return tgt.at[idx].add(src)

def _segment_sum(src, seg, n):
    return jax.ops.segment_sum(src, seg, n)
kernel_name = 'mk_xattn_ffn_d1_seqx_r4_f427bd'

def setup_inputs(seed: int=0):
    np.random.seed(seed)
    _w = jnp.asarray

    def _rec_inputs():
        import jax
        import jax.numpy as jnp
        _rk = jax.random.key(seed)
        x = -0.0002928 + 1 * jax.random.normal(jax.random.fold_in(_rk, 1), (16, 128, 256), jnp.float32)
        _lenS = 128 - jax.random.randint(jax.random.fold_in(_rk, 7), (16,), 0, max(1, 128 // 4) + 1, jnp.int32)
        _lenS2 = 128 - jax.random.randint(jax.random.fold_in(_rk, 8), (16,), 0, max(1, 128 // 4) + 1, jnp.int32)
        _ctx_1024P = jax.random.normal(jax.random.fold_in(_rk, 11), (16, 16, 256), jnp.float32)
        _ctx_1024c = jax.random.dirichlet(jax.random.fold_in(_rk, 511), 0.3 * jnp.ones((16,), jnp.float32), (16, 128))
        _ctx_1024t = jnp.einsum('bsk,bkd->bsd', _ctx_1024c, _ctx_1024P)
        _ctx_1024t = _ctx_1024t * jax.lax.rsqrt(jnp.mean(jnp.square(_ctx_1024t)) + 1e-12) * 0.953939
        ctx_1024 = -1.39393e-06 + 0.999914 * (_ctx_1024t + 0.3 * jax.random.normal(jax.random.fold_in(_rk, 611), (16, 128, 256), jnp.float32))
        return (x, ctx_1024)
    x, ctx_1024 = _rec_inputs()

    def _L0_xattn_setup():
        import jax, jax.numpy as jnp
        import numpy as np
        EMBED = 256
        HEADS = 16
        HIDDEN = 256
        HEAD_DIM = EMBED // HEADS
        key = jax.random.key(seed)
        ks = jax.random.split(key, 9)
        s = 1.0 / np.sqrt(HIDDEN)
        return {'q': jax.random.normal(ks[0], (2, 512, HIDDEN), jnp.float32), 'k': jax.random.normal(ks[1], (2, 512, HIDDEN), jnp.float32), 'v': jax.random.normal(ks[2], (2, 512, HIDDEN), jnp.float32), 'wq': jax.random.normal(ks[3], (HIDDEN, EMBED), jnp.float32) * s, 'bq': jax.random.normal(ks[4], (EMBED,), jnp.float32) * s, 'wk': jax.random.normal(ks[5], (HIDDEN, EMBED), jnp.float32) * s, 'bk': jax.random.normal(ks[6], (EMBED,), jnp.float32) * s, 'wv': jax.random.normal(ks[7], (HIDDEN, EMBED), jnp.float32) * s, 'bv': jax.random.normal(ks[8], (EMBED,), jnp.float32) * s}
    _L0_xattn_all = _L0_xattn_setup()
    _L0_xattn_in = {k: v for k, v in _L0_xattn_all.items() if k in ('wq', 'bq', 'wk', 'bk', 'wv', 'bv')}
    del _L0_xattn_all

    def _L0_ffn_setup():
        import jax, jax.numpy as jnp
        import numpy as np
        N_EMBED = 256
        FFN_HIDDEN = 1024
        NUM_EXPERTS = 8
        TOP_K = 2
        key = jax.random.key(seed)
        ks = jax.random.split(key, 8)
        d, f, E = (N_EMBED, FFN_HIDDEN, NUM_EXPERTS)
        s_d = 1.0 / np.sqrt(d)
        s_f = 1.0 / np.sqrt(f)
        return {'x': jax.random.normal(ks[0], (2, 512, d), dtype=jnp.float32), 'Wg': jax.random.uniform(ks[1], (d, E), jnp.float32, -s_d, s_d), 'bg': jax.random.uniform(ks[2], (E,), jnp.float32, -s_d, s_d), 'W1': jax.random.uniform(ks[3], (E, d, f), jnp.float32, -s_d, s_d), 'b1': jax.random.uniform(ks[4], (E, f), jnp.float32, -s_d, s_d), 'W2': jax.random.uniform(ks[5], (E, f, d), jnp.float32, -s_f, s_f), 'b2': jax.random.uniform(ks[6], (E, d), jnp.float32, -s_f, s_f)}
    _L0_ffn_all = _L0_ffn_setup()
    _L0_ffn_in = {k: v for k, v in _L0_ffn_all.items() if k in ('Wg', 'bg', 'W1', 'b1', 'W2', 'b2')}
    del _L0_ffn_all
    return {'x': x, 'ctx_1024': ctx_1024, 'L0_xattn_wq': _L0_xattn_in['wq'], 'L0_xattn_bq': _L0_xattn_in['bq'], 'L0_xattn_wk': _L0_xattn_in['wk'], 'L0_xattn_bk': _L0_xattn_in['bk'], 'L0_xattn_wv': _L0_xattn_in['wv'], 'L0_xattn_bv': _L0_xattn_in['bv'], 'L0_ffn_Wg': _L0_ffn_in['Wg'], 'L0_ffn_bg': _L0_ffn_in['bg'], 'L0_ffn_W1': _L0_ffn_in['W1'], 'L0_ffn_b1': _L0_ffn_in['b1'], 'L0_ffn_W2': _L0_ffn_in['W2'], 'L0_ffn_b2': _L0_ffn_in['b2']}

def reference(x, ctx_1024, L0_xattn_wq, L0_xattn_bq, L0_xattn_wk, L0_xattn_bk, L0_xattn_wv, L0_xattn_bv, L0_ffn_Wg, L0_ffn_bg, L0_ffn_W1, L0_ffn_b1, L0_ffn_W2, L0_ffn_b2):
    import jax
    import jax.numpy as jnp

    def _L0_xattn_ref(q, k, v, wq, bq, wk, bk, wv, bv):
        import jax, jax.numpy as jnp
        import numpy as np
        EMBED = 256
        HEADS = 16
        HIDDEN = 256
        HEAD_DIM = EMBED // HEADS
        B = q.shape[0]

        def split_heads(x):
            return x.reshape(B, -1, HEADS, HEAD_DIM).transpose(0, 2, 1, 3)
        qh = split_heads(q @ wq + bq)
        kh = split_heads(k @ wk + bk)
        vh = split_heads(v @ wv + bv)
        scale = 1.0 / np.sqrt(HEAD_DIM).astype(np.float32)
        scores = jnp.einsum('bhqd,bhkd->bhqk', qh, kh) * scale
        probs = jax.nn.softmax(scores, axis=-1)
        out = jnp.einsum('bhqk,bhkd->bhqd', probs, vh)
        return out.transpose(0, 2, 1, 3).reshape(B, -1, EMBED)

    def _L0_ffn_ref(x, Wg, bg, W1, b1, W2, b2):
        import jax, jax.numpy as jnp
        import numpy as np
        N_EMBED = 256
        FFN_HIDDEN = 1024
        NUM_EXPERTS = 8
        TOP_K = 2
        gate_scores = jax.nn.softmax(x @ Wg + bg, axis=-1)
        topk_scores, topk_idx = jax.lax.top_k(gate_scores, TOP_K)
        topk_scores = topk_scores / (jnp.sum(topk_scores, axis=-1, keepdims=True) + 1e-08)
        onehot = jax.nn.one_hot(topk_idx, NUM_EXPERTS, dtype=x.dtype)
        combine_w = jnp.einsum('bsk,bske->bse', topk_scores, onehot)
        output = jnp.zeros_like(x)
        for e in range(NUM_EXPERTS):
            h = jax.nn.gelu(x @ W1[e] + b1[e])
            y = h @ W2[e] + b2[e]
            output = output + y * combine_w[..., e:e + 1]
        return output
    x = x + _L0_xattn_ref(_layernorm(x, axis=-1), ctx_1024, ctx_1024, L0_xattn_wq, L0_xattn_bq, L0_xattn_wk, L0_xattn_bk, L0_xattn_wv, L0_xattn_bv)
    x = x + _L0_ffn_ref(_layernorm(x, axis=-1), L0_ffn_Wg, L0_ffn_bg, L0_ffn_W1, L0_ffn_b1, L0_ffn_W2, L0_ffn_b2)
    return x

_drawn_inputs = setup_inputs


def setup_inputs(seed=0):
    import zlib

    import numpy as np

    out = dict(_drawn_inputs(seed))
    spreads = {}
    factors = {'L0_xattn_bq': 3.251, 'L0_xattn_bk': 8.0, 'L0_ffn_b1': 6.962, 'L0_ffn_b2': 4.934}
    for name, (base, spread) in spreads.items():
        noise = np.random.default_rng([zlib.crc32(name.encode()), seed]).standard_normal(out[name].shape)
        drawn = base * np.exp(spread * noise) if base else spread * noise
        out[name] = jnp.asarray(drawn.astype(out[name].dtype))
    for name, factor in factors.items():
        out[name] = (out[name] * factor).astype(out[name].dtype)
    return out
```

```python
from contextlib import ExitStack

import concourse.bass as bass
from concourse import mybir

P = 128
ALU = mybir.AluOpType
ACT = mybir.ActivationFunctionType
AX_X = mybir.AxisListType.X
F32 = mybir.dt.float32
F16 = mybir.dt.float16
BF16 = mybir.dt.bfloat16
I32 = mybir.dt.int32


def build_xattn_moe(nc, x, ctx_in, wq, bq, wk, bk, wv, bv, wg, bg, w1, b1, w2, b2, out):
    NB, S, D = x.shape
    NE, _, F = w1.shape
    HEADS = 16
    HD = D // HEADS
    DC = D // P
    FC = F // P
    HC = HEADS // DC
    GH = 4
    NG = HEADS // GH
    VW = 32
    U = 4
    NU = NB // U
    N = NB * S
    TPE = N // P
    ITEM = 2 * P
    ROW = D + NE
    SKIP = 2 * N
    SCALE = 1.0 / HD ** 0.5
    TOPK = 2
    assert S == P and NU >= 2 and NE == 8

    x_v = x.rearrange("b s d -> s b d")
    out_v = out
    out_rows = out.rearrange("b s d -> (b s) d")
    w1_v = w1.rearrange("e (c p) f -> e p c f", p=P)
    w2_v = w2.rearrange("e (c p) d -> e p c d", p=P)
    table = nc.dram_tensor("token_table", [N, ROW], F32).ap()
    table_v = table.rearrange("(b s) d -> b s d", s=S)

    with ExitStack() as stack:
        def sb(name, shape, dt=F32):
            return stack.enter_context(nc.sbuf_tensor(name, shape, dt))

        def sem(name):
            return stack.enter_context(nc.semaphore(name))

        ident = sb("ident", [P, P])
        head_mask = sb("head_mask", [P, HC])
        earlier = sb("earlier", [P, P], BF16)
        ones_bf = sb("ones_bf", [P, P], BF16)
        iota_s = sb("iota_s", [P, P])
        iota_c = sb("iota_c", [P, P])
        codes = sb("codes", [P, U, NE])
        iota_i = sb("iota_i", [P, P], I32)
        codes_i = sb("codes_i", [P, U, NE], I32)
        tok_i = sb("tok_i", [P, NB], I32)
        tok1 = sb("tok1", [P, NB])
        minus_half = sb("minus_half", [P, NB])
        wq_sb = sb("wq_sb", [P, DC, D])
        wk_sb = sb("wk_sb", [P, DC, D])
        wv_sb = sb("wv_sb", [P, DC, D])
        wg_sb = sb("wg_sb", [P, DC, NE])
        bv_bc = sb("bv_bc", [P, D])
        bg_bc = sb("bg_bc", [P, NE])
        b2_bc = sb("b2_bc", [P, NE, D])
        NBR = NE * FC + 2 * DC
        bias_rows = sb("bias_rows", [NBR, P])
        bias_cols = sb("bias_cols", [P, NBR])

        x_all = sb("x_all", [P, NB, D])
        ctx_sb = sb("ctx_sb", [P, D])
        stats = sb("stats", [P, U, 6])
        mv = sb("mv", [P, U, 2])
        mean = sb("mean", [P, NB])
        rstd = sb("rstd", [P, NB])
        vare = sb("vare", [P, NB])
        xn = sb("xn", [P, D])
        xcT = sb("xcT", [P, 2 * DC, P])
        qkT = sb("qkT", [P, 2 * DC, P])
        kmask = sb("kmask", [P, DC, HC, P])
        v_ext = sb("v_ext", [P, HEADS, VW])
        negmax = sb("negmax", [P, HEADS])
        probs = sb("probs", [P, HEADS, P])
        pT = sb("pT", [P, 2, GH, P])
        oT_sb = sb("oT_sb", [P, NG, P])
        inv_sum = sb("inv_sum", [P, HEADS])
        att = sb("att", [P, D])
        x1 = sb("x1", [P, D])
        stats2 = sb("stats2", [P, 6])
        mv2 = sb("mv2", [P, 2])
        vare2 = sb("vare2", [P, 1])
        rstd2 = sb("rstd2", [P, 1])
        xn2 = sb("xn2", [P, D])
        xn2T = sb("xn2T", [P, DC, P])
        lg = sb("lg", [P, U, NE])
        lgs = sb("lgs", [P, U, NE])
        ex = sb("ex", [P, U, NE])
        pr = sb("pr", [P, U, NE])
        pr2 = sb("pr2", [P, U, NE])
        eq = sb("eq", [P, U, NE])
        t4 = sb("t4", [P, 4, U])
        top = sb("top", [P, TOPK, U])
        code = sb("code", [P, TOPK, U])
        onehot = sb("onehot", [P, TOPK, U, NE])
        ohr = sb("ohr", [P, TOPK, U, NE])
        ohw = sb("ohw", [P, TOPK, U, NE])
        wtop = sb("wtop", [P, TOPK, U])
        cw = sb("cw", [P, U, NE])
        picked = sb("picked", [P, U, NE], BF16)
        before = sb("before", [P, U, NE], BF16)
        run = sb("run", [P, NE], BF16)
        rank = sb("rank", [P, TOPK, U])
        rank_i = sb("rank_i", [P, TOPK, U], I32)
        tile_i = sb("tile_i", [P, TOPK, U], I32)
        slot_i = sb("slot_i", [P, TOPK, U], I32)
        slot_f = sb("slot_f", [P, TOPK, U])
        col_f = sb("col_f", [P, TOPK, U])
        hot_s = sb("hot_s", [P, TOPK * U, P], F16)
        hot_c = sb("hot_c", [P, TOPK * U, P], F16)
        ids = sb("ids", [P, NE * TPE])
        ids_f = sb("ids_f", [P, NE * TPE])
        ids_get = sb("ids_get", [P, NE * TPE], I32)
        ids_put = sb("ids_put", [P, NE * TPE], I32)
        cnt_f = sb("cnt_f", [P, NE])
        cnt_i = sb("cnt_i", [P, NE], I32)
        items = sb("items", [P, NE], I32)
        w1_sb = [sb(f"w1_sb{i}", [P, DC, F]) for i in range(2)]
        w2_sb = [sb(f"w2_sb{i}", [P, FC, D]) for i in range(2)]
        get_idx = sb("get_idx", [P, 2], I32)
        put_new = sb("put_new", [P, 2], I32)
        put_next = sb("put_next", [P, 2], I32)
        put_idx = sb("put_idx", [P, 2], I32)
        rows0 = sb("rows0", [P, ROW])
        rows1 = sb("rows1", [P, ROW])
        rows = [rows0, rows1]
        cw_next = sb("cw_next", [P, 2, NE])
        cw_now = sb("cw_now", [P, 2, NE])
        xT = sb("xT", [P, DC, ITEM])
        hT = sb("hT", [P, FC, ITEM])
        yb = sb("yb", [P, 2, D])
        yw0 = sb("yw0", [P, D])
        yw1 = sb("yw1", [P, D])
        yw = [yw0, yw1]

        ps = stack.enter_context(nc.psum_tensor("ps", [P, 8, 512], F32))
        PT, OB, MB = 4, 6, 7
        RK = D

        x_in = [sem("x_in_first"), sem("x_in_rest")]
        ctx_s = sem("ctx_loaded")
        wts_in = sem("attn_weights_loaded")
        small_in = sem("bias_rows_loaded")
        bcast_in = sem("broadcast_biases_loaded")
        consts = sem("constants_built")
        pool_step = sem("pool_step")
        bias_ps = sem("biases_transposed")
        dve_step = sem("dve_step")
        stats_done = sem("ln1_stats_done")
        rstd_done = sem("ln1_rstd_done")
        xn_done = sem("xn_done")
        xcT_ps = sem("xcT_in_psum")
        xcT_sb = sem("xcT_in_sbuf")
        qk_ps = sem("qk_in_psum")
        qk_sb = sem("qk_in_sbuf")
        v_ps = sem("v_in_psum")
        v_sb = sem("v_in_sbuf")
        kmask_s = sem("kmask_done")
        s_ps = sem("scores_in_psum")
        max_s = sem("negmax_done")
        exp_s = sem("probs_done")
        pT_ps = sem("pT_in_psum")
        pT_dve = sem("pT_copied_by_dve")
        pT_act = sem("pT_copied_by_act")
        pv_s = sem("pv_in_psum")
        o_sb = sem("oT_in_sbuf")
        o_ps = sem("o_in_psum")
        x1_s = sem("x1_done")
        x1_out = sem("x1_stored")
        var2_s = sem("ln2_var_done")
        rstd2_s = sem("ln2_rstd_done")
        xn2_s = sem("xn2_done")
        xn2_out = sem("xn2_stored")
        xn2T_ps = sem("xn2T_in_psum")
        xn2T_sb = sem("xn2T_in_sbuf")
        lg_ps = sem("logits_in_psum")
        lg_read = sem("logits_read")
        lg_s = sem("logits_shifted")
        ex_s = sem("router_exp_done")
        cw_s = sem("combine_weights_done")
        cw_out = sem("combine_weights_stored")
        pick_s = sem("choices_done")
        rank_read = sem("ranks_read")
        rank_ps = sem("ranks_in_psum")
        hot_s_done = sem("onehots_done")
        ids_ps = sem("ids_in_psum")
        ids_s = sem("ids_added")
        run_s = sem("totals_done")
        cnt_ps = sem("counts_in_psum")
        lists = sem("lists_ready")
        w_in = [sem("ffn_weights0_loaded"), sem("ffn_weights1_loaded")]
        idx_s = sem("gather_indices_copied")
        gat = sem("rows_gathered")
        xt_ps = sem("item_transposed")
        xt_sb = sem("item_in_sbuf")
        h_ps = sem("hidden_in_psum")
        h_sb = sem("hidden_in_sbuf")
        y_ps = sem("y_in_psum")
        y_b = sem("y_biased")
        y_s = sem("y_scaled")
        cw_moved = sem("cw_moved")
        put_s = sem("rows_added")
        put_q = sem("put_queue_moved")

        block = stack.enter_context(nc.Block())

        wait_registers = {}

        def wait_alone(eng, signal, value):
            if not isinstance(value, int):
                if eng.engine not in wait_registers:
                    wait_registers[eng.engine] = eng.alloc_register(f"wait_value_{len(wait_registers)}")
                eng.reg_mov(wait_registers[eng.engine], value)
                value = wait_registers[eng.engine]
            eng.wait_ge(consts, 1)
            eng.wait_ge(signal, value)

        def groups(eng, body):
            body(0, False)
            with eng.Fori(1, NU - 1) as q:
                body(q, False)
            body(NU - 1, True)

        @block.sync
        def _(sp):
            sp.dma_start(x_all[:, 0:U, :], x_v[:, 0:U, :]).then_inc(x_in[0], 16)
            sp.dma_start(ctx_sb[:], ctx_in[0]).then_inc(ctx_s, 16)
            sp.dma_start(x_all[:, U:, :], x_v[:, U:, :]).then_inc(x_in[1], 16)
            for b in range(2):
                sp.wait_ge(xcT_ps, b + 1)
                sp.dma_start(ctx_sb[:], ctx_in[b + 1]).then_inc(ctx_s, 16)

            def store_cw(q):
                sp.wait_ge(cw_s, q + 1)
                sp.dma_start(table_v[bass.ds(q * U, U), :, D:ROW].rearrange("b s e -> s b e"),
                             cw[:]).then_inc(cw_out, 16)

            def body(q, last):
                for u in range(U):
                    b = q * U + u
                    sp.wait_ge(x1_s, b + 1)
                    sp.dma_start(out_v[bass.ds(b, 1)].rearrange("o s d -> (o s) d"), x1[:]).then_inc(x1_out, 16)
                    sp.wait_ge(xn2_s, b + 1)
                    sp.dma_start(table_v[bass.ds(b, 1), :, 0:D].rearrange("o s d -> (o s) d"),
                                 xn2[:]).then_inc(xn2_out, 16)
                    if not (last and u >= U - 3):
                        sp.wait_ge(xcT_ps, b + 3)
                        sp.dma_start(ctx_sb[:], ctx_in[bass.ds(b + 3, 1)].rearrange("o s d -> (o s) d")
                                     ).then_inc(ctx_s, 16)
                    if u == 3 and not (isinstance(q, int) and q == 0):
                        store_cw(q - 1)
            groups(sp, body)
            store_cw(NU - 1)

            sp.wait_ge(x1_out, NB * 16)
            sp.wait_ge(xn2_out, NB * 16)
            sp.wait_ge(cw_out, NU * 16)
            sp.wait_ge(lists, 1)
            done = sp.alloc_register("sp_items_done")
            sp.reg_mov(done, 0)
            with sp.Fori(0, NE // 2 - 1) as pair:
                for par in range(2):
                    n = sp.value_load(items[0:1, bass.ds(pair * 2 + par, 1)], min_val=1, max_val=N // ITEM)
                    sp.reg_add(done, done, n)
                    sp.wait_ge(y_ps, sp.snap(done))
                    e = pair * 2 + (par + 2)
                    sp.dma_start(w1_sb[par][:], w1_v[bass.ds(e, 1)].rearrange("o p c f -> (o p) c f")
                                 ).then_inc(w_in[par], 16)
                    sp.dma_start(w2_sb[par][:], w2_v[bass.ds(e, 1)].rearrange("o p c d -> (o p) c d")
                                 ).then_inc(w_in[par], 16)
            for par in range(2):
                n = sp.value_load(items[0:1, NE - 2 + par:NE - 1 + par], min_val=1, max_val=N // ITEM)
                sp.reg_add(done, done, n)
            total = sp.snap(done)
            wait_alone(sp, put_s, (total + 3) * 32)

        @block.tensor
        def _(pe):
            def rank_group(q):
                pe.wait_ge(pick_s, q + 1)
                rk = ps[:, MB, RK:RK + U * NE]
                pe.matmul(rk, earlier[:], picked[:].rearrange("p u e -> p (u e)"), start=True, stop=False)
                pe.matmul(rk, ones_bf[:], before[:].rearrange("p u e -> p (u e)"), start=False, stop=True
                          ).then_inc(rank_ps, 1)

            def place_ids(q):
                pe.wait_ge(hot_s_done, q + 1)
                for k in range(TOPK * U):
                    m = pe.matmul(ps[:, MB, 384:512], hot_s[:, k, :], hot_c[:, k, :],
                                  start=(k == 0), stop=(k == TOPK * U - 1))
                m.then_inc(ids_ps, 1)

            def prep(b):
                pe.wait_ge(consts, 1)
                pe.wait_ge(xn_done, b + 1)
                pe.wait_ge(ctx_s, (b + 1) * 16)
                if isinstance(b, int) and b == 0:
                    pass
                else:
                    pe.wait_ge(v_sb, b)
                for j in range(2 * DC):
                    src = xn if j < DC else ctx_sb
                    m = pe.transpose(ps[:, MB, j * P:(j + 1) * P], src[:, (j % DC) * P:(j % DC + 1) * P], ident[:])
                m.then_inc(xcT_ps, 1)
                pe.wait_ge(xcT_sb, b + 1)
                if isinstance(b, int) and b == 0:
                    pe.wait_ge(wts_in, 64)
                for j in range(2 * DC):
                    w = wq_sb if j < DC else wk_sb
                    src = 0 if j < DC else DC
                    for c in range(DC):
                        m = pe.matmul(ps[:, OB, j * P:(j + 1) * P], w[:, c, (j % DC) * P:(j % DC + 1) * P],
                                      xcT[:, src + c, :], start=(c == 0), stop=(c == DC - 1))
                m.then_inc(qk_ps, 1)
                for c in range(DC):
                    m = pe.matmul(ps[:, MB, 0:D], xcT[:, DC + c, :], wv_sb[:, c, :],
                                  start=(c == 0), stop=(c == DC - 1))
                m.then_inc(v_ps, 1)

            def scores(b):
                pe.wait_ge(qk_sb, b + 1)
                for c in range(DC):
                    pe.wait_ge(kmask_s, b * DC + c + 1)
                    for g in range(HC // GH):
                        m = pe.matmul(ps[:, c * (HC // GH) + g, :], qkT[:, c, :],
                                      kmask[:, c, g * GH:(g + 1) * GH, :], start=True, stop=True)
                    m.then_inc(s_ps, 1)

            def turn_probs(b, g):
                pe.wait_ge(exp_s, b * NG + g + 1)
                if g >= 2:
                    pe.wait_ge(pT_act if g % 2 else pT_dve, b * (NG // 2) + g // 2)
                elif g == 1 and not (isinstance(b, int) and b == 0):
                    pe.wait_ge(lg_read, b)
                for i in range(GH):
                    m = pe.transpose(ps[:, PT + g % 2, i * P:(i + 1) * P], probs[:, g * GH + i, :], ident[:])
                m.then_inc(pT_ps, 1)

            def times_v(b, g, more1):
                pe.wait_ge(pT_act if g % 2 else pT_dve, b * (NG // 2) + g // 2 + 1)
                if g == 0:
                    pe.wait_ge(v_sb, b + 1)
                    if more1:
                        pe.wait_ge(qk_sb, b + 2)
                for i in range(GH):
                    m = pe.matmul(ps[i * VW:(i + 1) * VW, OB, g * P:(g + 1) * P],
                                  v_ext[:, g * GH + i, :], pT[:, g % 2, i, :], start=True, stop=True,
                                  tile_position=(0, i * VW))
                m.then_inc(pv_s, 1)

            def body(q, last):
                for u in range(U):
                    b = q * U + u
                    more1 = not (last and u >= U - 1)
                    more2 = not (last and u >= U - 2)
                    turn_probs(b, 0)
                    turn_probs(b, 1)
                    for g in range(NG):
                        times_v(b, g, more1)
                        if g + 2 < NG:
                            turn_probs(b, g + 2)
                    if more1:
                        scores(b + 1)
                    pe.wait_ge(o_sb, b + 1)
                    for g in range(NG):
                        m = pe.transpose(ps[:, PT, g * P:(g + 1) * P], oT_sb[:, g, :], ident[:])
                    m.then_inc(o_ps, 1)
                    if more2:
                        if u == 2 and not (isinstance(q, int) and q == 0):
                            pe.wait_ge(rank_read, q)
                        if u == 3 and not (isinstance(q, int) and q == 0):
                            pe.wait_ge(ids_s, q)
                        prep(b + 2)
                    pe.wait_ge(xn2_s, b + 1)
                    for c in range(DC):
                        m = pe.transpose(ps[:, PT + 1, c * P:(c + 1) * P], xn2[:, c * P:(c + 1) * P], ident[:])
                    m.then_inc(xn2T_ps, 1)
                    pe.wait_ge(xn2T_sb, b + 1)
                    for c in range(DC):
                        m = pe.matmul(ps[:, PT + 1, D + u * NE:D + (u + 1) * NE], xn2T[:, c, :], wg_sb[:, c, :],
                                      start=(c == 0), stop=(c == DC - 1))
                    m.then_inc(lg_ps, 1)
                    if u == 1 and not (isinstance(q, int) and q == 0):
                        rank_group(q - 1)
                    if u == 2 and not (isinstance(q, int) and q == 0):
                        place_ids(q - 1)

            pe.wait_ge(consts, 1)
            pe.wait_ge(small_in, 48)
            pe.transpose(ps[:, PT, 0:NBR], bias_rows[:], ident[0:NBR, 0:NBR]).then_inc(bias_ps, 1)
            prep(0)
            scores(0)
            prep(1)
            groups(pe, body)
            rank_group(NU - 1)
            place_ids(NU - 1)
            pe.wait_ge(run_s, 1)
            pe.matmul(ps[:, PT + 1, 0:NE], ones_bf[:], run[:], start=True, stop=True).then_inc(cnt_ps, 1)

            g = pe.alloc_register("pe_item")
            pe.reg_mov(g, 1)
            chunks = pe.alloc_register("pe_chunks")
            pe.reg_mov(chunks, 0)

            def turn_item(k):
                pe.wait_ge(gat, k * 32)
                pe.wait_ge(xt_sb, k)
                for half in range(2):
                    for c in range(DC):
                        m = pe.transpose(ps[:, OB, c * ITEM + half * P:c * ITEM + (half + 1) * P],
                                         rows[half][:, c * P:(c + 1) * P], ident[:])
                m.then_inc(xt_ps, 1)

            pe.wait_ge(lists, 1)
            turn_item(1)
            with pe.Fori(0, NE // 2) as pair:
                for par in range(2):
                    n = pe.value_load(items[0:1, bass.ds(pair * 2 + par, 1)], min_val=1, max_val=N // ITEM)
                    wait_alone(pe, w_in[par], pair * 32 + 32)
                    with pe.Fori(0, n) as _i:
                        k = pe.snap(g)
                        hc = pe.snap(chunks)
                        pe.wait_ge(xt_sb, k + 1)
                        for f in range(FC):
                            if f >= 4:
                                pe.wait_ge(h_sb, hc + f - 3)
                            for c in range(DC):
                                m = pe.matmul(ps[:, f % 4, 0:ITEM], w1_sb[par][:, c, f * P:(f + 1) * P],
                                              xT[:, c, :], start=(c == 0), stop=(c == DC - 1))
                            m.then_inc(h_ps, 1)
                        turn_item(k + 1)
                        pe.wait_ge(y_s, k + 1)
                        for f in range(FC):
                            pe.wait_ge(h_sb, hc + f + 1)
                            for half in range(2):
                                m = pe.matmul(ps[:, PT + half, 0:D], hT[:, f, half * P:(half + 1) * P],
                                              w2_sb[par][:, f, :], start=(f == 0), stop=(f == FC - 1))
                        m.then_inc(y_ps, 1)
                        pe.reg_add(g, g, 1)
                        pe.reg_add(chunks, chunks, FC)

        @block.scalar
        def _(act):
            act.dma_start(bias_rows[0:NE * FC, :], b1.rearrange("e (f p) -> (e f) p", p=P)).then_inc(small_in, 16)
            act.dma_start(bias_rows[NE * FC:NE * FC + DC, :], bq.rearrange("(c p) -> c p", p=P)).then_inc(small_in, 16)
            act.dma_start(bias_rows[NE * FC + DC:NBR, :], bk.rearrange("(c p) -> c p", p=P)).then_inc(small_in, 16)
            act.dma_start(wq_sb[:], wq.rearrange("(c p) n -> p c n", p=P)).then_inc(wts_in, 16)
            act.dma_start(wk_sb[:], wk.rearrange("(c p) n -> p c n", p=P)).then_inc(wts_in, 16)
            act.dma_start(wv_sb[:], wv.rearrange("(c p) n -> p c n", p=P)).then_inc(wts_in, 16)
            act.dma_start(wg_sb[:], wg.rearrange("(c p) n -> p c n", p=P)).then_inc(wts_in, 16)
            act.dma_start(bv_bc[:], bv.partition_broadcast(P)).then_inc(bcast_in, 16)
            act.dma_start(bg_bc[:], bg.partition_broadcast(P)).then_inc(bcast_in, 16)
            act.dma_start(b2_bc[:], b2.partition_broadcast(P)).then_inc(bcast_in, 16)
            for par in range(2):
                act.dma_start(w1_sb[par][:], w1_v[par]).then_inc(w_in[par], 16)
                act.dma_start(w2_sb[par][:], w2_v[par]).then_inc(w_in[par], 16)

            def copy_xcT(b):
                act.wait_ge(xcT_ps, b + 1)
                act.copy(xcT[:], ps[:, MB, :].rearrange("p (j n) -> p j n", j=2 * DC)).then_inc(xcT_sb, 1)

            def router_exp(q):
                act.wait_ge(lg_s, q + 1)
                act.activation(ex[:], lgs[:], ACT.Exp).then_inc(ex_s, 1)

            def exp_probs(b, chunks=range(DC)):
                for c in chunks:
                    act.wait_ge(max_s, b * DC + c + 1)
                    for h in range(c * HC, (c + 1) * HC):
                        m = act.activation(probs[:, h, :], ps[:, h // GH, (h % GH) * P:(h % GH + 1) * P], ACT.Exp,
                                           bias=negmax[:, h:h + 1])
                        if h % GH == GH - 1:
                            m.then_inc(exp_s, 1)

            def body(q, last):
                for u in range(U):
                    b = q * U + u
                    for g in (1, 3):
                        act.wait_ge(pT_ps, b * NG + g + 1)
                        if g == 3:
                            act.wait_ge(pv_s, b * NG + 2)
                        act.copy(pT[:, 1, :, :], ps[:, PT + 1, :].rearrange("p (i n) -> p i n", i=GH)
                                 ).then_inc(pT_act, 1)
                    act.wait_ge(pv_s, (b + 1) * NG)
                    act.copy(oT_sb[:], ps[:, OB, :].rearrange("p (g n) -> p g n", g=NG)).then_inc(o_sb, 1)
                    if not (last and u >= U - 1):
                        exp_probs(b + 1, [0])
                    if not (last and u >= U - 2):
                        copy_xcT(b + 2)
                    if not (last and u >= U - 1):
                        exp_probs(b + 1, range(1, DC))
                    act.wait_ge(xn2T_ps, b + 1)
                    act.copy(xn2T[:], ps[:, PT + 1, 0:D].rearrange("p (c n) -> p c n", c=DC)).then_inc(xn2T_sb, 1)
                    if u == 0 and not (isinstance(q, int) and q == 0):
                        router_exp(q - 1)

            copy_xcT(0)
            exp_probs(0)
            copy_xcT(1)
            groups(act, body)
            router_exp(NU - 1)

            g = act.alloc_register("act_chunks")
            act.reg_mov(g, 0)
            act.wait_ge(lists, 1)
            with act.Fori(0, NE) as e:
                n = act.value_load(items[0:1, bass.ds(e, 1)], min_val=1, max_val=N // ITEM)
                with act.Fori(0, n) as _i:
                    k = act.snap(g)
                    for f in range(FC):
                        act.wait_ge(h_ps, k + f + 1)
                        act.activation(hT[:, f, :], ps[:, f % 4, 0:ITEM], ACT.Gelu_apprx_tanh,
                                       bias=bias_cols[:, bass.ds(e * FC + f, 1)]).then_inc(h_sb, 1)
                    act.reg_add(g, g, FC)

        @block.vector
        def _(dve):
            PER_GROUP = 2 * U + 1 + 4 * U + 31
            step = [0]
            base = [0]

            def did(m):
                step[0] += 1
                m.then_inc(dve_step, 1)

            def settle(own=False):
                if own:
                    wait_alone(dve, dve_step, base[0] + step[0])
                else:
                    dve.wait_ge(dve_step, base[0] + step[0])

            def ln1_stats(q):
                for u in range(U):
                    did(dve.bn_stats(stats[:, u, :],
                                     x_all[:, bass.ds(q * U + u, 1), :].rearrange("p o d -> p (o d)")))
                settle(own=True)
                for u in range(U):
                    did(dve.bn_aggr(mv[:, u, :], stats[:, u, :]))
                settle()
                did(dve.tensor_copy(mean[:, bass.ds(q * U, U)], mv[:, :, 0:1].rearrange("p b o -> p (b o)")))
                dve.tensor_scalar(vare[:, bass.ds(q * U, U)], mv[:, :, 1:2].rearrange("p b o -> p (b o)"),
                                  1e-5, None, ALU.add).then_inc(stats_done, 1)

            def normalise(b, q):
                dve.wait_ge(rstd_done, q + 1)
                if isinstance(b, int) and b == 0:
                    pass
                else:
                    dve.wait_ge(xcT_ps, b)
                dve.tensor_scalar(xn[:], x_all[:, bass.ds(b, 1), :].rearrange("p o d -> p (o d)"),
                                  mean[:, bass.ds(b, 1)], rstd[:, bass.ds(b, 1)],
                                  ALU.subtract, ALU.mult).then_inc(xn_done, 1)

            def copy_qk(b):
                dve.wait_ge(qk_ps, b + 1)
                if not (isinstance(b, int) and b == 0):
                    dve.wait_ge(s_ps, b * DC)
                    dve.wait_ge(kmask_s, b * DC)
                dve.tensor_tensor(qkT[:], ps[:, OB, :].rearrange("p (j n) -> p j n", j=2 * DC),
                                  bias_cols[:, NE * FC:NBR].unsqueeze(2).to_broadcast([P, 2 * DC, P]),
                                  ALU.add).then_inc(qk_sb, 1)

            def copy_v(b):
                dve.wait_ge(v_ps, b + 1)
                if not (isinstance(b, int) and b == 0):
                    dve.wait_ge(pv_s, b * NG)
                dve.tensor_tensor(v_ext[:, :, 0:HD], ps[:, MB, 0:D].rearrange("p (h n) -> p h n", h=HEADS),
                                  bv_bc[:].rearrange("p (h n) -> p h n", h=HEADS), ALU.add).then_inc(v_sb, 1)

            def row_max(b, c):
                dve.wait_ge(s_ps, b * DC + c + 1)
                if c == 0 and not (isinstance(b, int) and b == 0):
                    dve.wait_ge(exp_s, b * NG)
                nb = HC // GH
                dve.tensor_reduce(negmax[:, c * HC:(c + 1) * HC],
                                  ps[:, c * nb:(c + 1) * nb, :].rearrange("p g (h n) -> p (g h) n", h=GH),
                                  AX_X, ALU.max, negate=True).then_inc(max_s, 1)

            def body(q, last):
                step[0] = 0
                base[0] = first_steps + (q * PER_GROUP if isinstance(q, int) and q == 0 else q * PER_GROUP - 31)
                if not last:
                    dve.wait_ge(x_in[1], 16)
                    ln1_stats(q + 1)
                for u in range(U):
                    b = q * U + u
                    more1 = not (last and u >= U - 1)
                    more2 = not (last and u >= U - 2)
                    if more2:
                        normalise(b + 2, q if u < U - 2 else q + 1)
                    for g in (0, 2):
                        dve.wait_ge(pT_ps, b * NG + g + 1)
                        if g == 2:
                            dve.wait_ge(pv_s, b * NG + 1)
                        dve.tensor_copy(pT[:, 0, :, :], ps[:, PT, :].rearrange("p (i n) -> p i n", i=GH)
                                        ).then_inc(pT_dve, 1)
                    if not (isinstance(q, int) and q == 0):
                        (no_route, no_route, route_ranks, route_add)[u](q - 1)
                    if more1:
                        copy_v(b + 1)
                        for c in range(DC):
                            row_max(b + 1, c)
                    dve.wait_ge(o_ps, b + 1)
                    o_v = ps[:, PT, :].rearrange("p (h w) -> p h w", w=VW)
                    did(dve.reciprocal(inv_sum[:], o_v[:, :, HD:HD + 1].rearrange("p h o -> p (h o)")))
                    settle()
                    did(dve.tensor_tensor(att[:].rearrange("p (h n) -> p h n", h=HEADS), o_v[:, :, 0:HD],
                                          inv_sum[:].unsqueeze(2).to_broadcast([P, HEADS, HD]), ALU.mult))
                    settle()
                    if not (isinstance(q, int) and q == 0 and u == 0):
                        dve.wait_ge(x1_out, b * 16)
                    dve.tensor_tensor(x1[:], att[:], x_all[:, bass.ds(b, 1), :].rearrange("p o d -> p (o d)"),
                                      ALU.add).then_inc(x1_s, 1)
                    dve.wait_ge(x1_s, b + 1)
                    did(dve.bn_stats(stats2[:], x1[:]))
                    settle(own=True)
                    did(dve.bn_aggr(mv2[:], stats2[:]))
                    settle()
                    dve.tensor_scalar(vare2[:], mv2[:, 1:2], 1e-5, None, ALU.add).then_inc(var2_s, 1)
                    dve.wait_ge(rstd2_s, b + 1)
                    if not (isinstance(q, int) and q == 0 and u == 0):
                        dve.wait_ge(xn2_out, b * 16)
                    dve.tensor_scalar(xn2[:], x1[:], mv2[:, 0:1], rstd2[:], ALU.subtract, ALU.mult).then_inc(xn2_s, 1)
                    if more2:
                        copy_qk(b + 2)
                    if not (isinstance(q, int) and q == 0):
                        (route_softmax, route_choose, route_place, no_route)[u](q - 1)
                    dve.wait_ge(lg_ps, b + 1)
                    dve.tensor_tensor(lg[:, u, :], ps[:, PT + 1, D + u * NE:D + (u + 1) * NE], bg_bc[:], ALU.add
                                      ).then_inc(lg_read, 1)

            def bc(ap):
                return ap.unsqueeze(2).to_broadcast([P, U, NE])

            def no_route(q):
                pass

            def route_softmax(q):
                dve.wait_ge(lg_read, (q + 1) * U)
                did(dve.tensor_reduce(t4[:, 0, :], lg[:], AX_X, ALU.max))
                settle()
                dve.tensor_tensor(lgs[:], lg[:], bc(t4[:, 0, :]), ALU.subtract).then_inc(lg_s, 1)
                dve.wait_ge(lg_s, q + 1)

            def route_choose(q):
                dve.wait_ge(ex_s, q + 1)
                did(dve.tensor_reduce(t4[:, 1, :], ex[:], AX_X, ALU.add))
                settle()
                did(dve.reciprocal(t4[:, 2, :], t4[:, 1, :]))
                settle()
                did(dve.tensor_tensor(pr[:], ex[:], bc(t4[:, 2, :]), ALU.mult))
                settle()
                src = pr
                for k in range(TOPK):
                    did(dve.tensor_reduce(top[:, k, :], src[:], AX_X, ALU.max))
                    settle()
                    did(dve.tensor_tensor(eq[:], src[:], bc(top[:, k, :]), ALU.is_equal))
                    settle()
                    did(dve.tensor_tensor(eq[:], eq[:], codes[:], ALU.mult))
                    settle()
                    did(dve.tensor_reduce(code[:, k, :], eq[:], AX_X, ALU.max))
                    settle()
                    did(dve.tensor_tensor(onehot[:, k], codes[:], bc(code[:, k, :]), ALU.is_equal))
                    settle()
                    if k == 0:
                        did(dve.scalar_tensor_tensor(pr2[:], onehot[:, 0], -2.0, pr[:], ALU.mult, ALU.add))
                        settle()
                        src = pr2
                if not (isinstance(q, int) and q == 0):
                    dve.wait_ge(rank_ps, q)
                did(dve.tensor_tensor(picked[:], onehot[:, 0], onehot[:, 1], ALU.add))
                did(dve.tensor_copy(before[:, 0, :], run[:]))
                settle()
                for u in range(1, U):
                    did(dve.tensor_tensor(before[:, u, :], before[:, u - 1, :], picked[:, u - 1, :], ALU.add))
                    settle()
                dve.tensor_tensor(run[:], before[:, U - 1, :], picked[:, U - 1, :], ALU.add).then_inc(pick_s, 1)

            def route_ranks(q):
                dve.wait_ge(rank_ps, q + 1)
                rk = ps[:, MB, RK:RK + U * NE].rearrange("p (u e) -> p u e", u=U)
                for k in range(TOPK):
                    m = dve.tensor_tensor(ohr[:, k], onehot[:, k], rk, ALU.mult)
                m.then_inc(rank_read, 1)
                dve.wait_ge(rank_read, q + 1)

            def route_place(q):
                did(dve.tensor_tensor(t4[:, 3, :], top[:, 0, :], top[:, 1, :], ALU.add))
                settle()
                did(dve.tensor_scalar(t4[:, 3, :], t4[:, 3, :], 1e-8, None, ALU.add))
                settle()
                did(dve.reciprocal(t4[:, 2, :], t4[:, 3, :]))
                settle()
                did(dve.tensor_tensor(wtop[:], top[:], t4[:, 2:3, :].to_broadcast([P, TOPK, U]), ALU.mult))
                settle()
                did(dve.tensor_tensor(ohw[:].rearrange("p k u e -> p (k u) e"),
                                      onehot[:].rearrange("p k u e -> p (k u) e"),
                                      wtop[:].rearrange("p k u -> p (k u)").unsqueeze(2).to_broadcast([P, TOPK * U, NE]),
                                      ALU.mult))
                settle()
                if not (isinstance(q, int) and q == 0):
                    dve.wait_ge(cw_out, q * 16)
                dve.tensor_tensor(cw[:], ohw[:, 0], ohw[:, 1], ALU.add).then_inc(cw_s, 1)
                did(dve.tensor_reduce(rank[:], ohr[:], AX_X, ALU.add))
                settle()
                did(dve.tensor_copy(rank_i[:], rank[:]))
                settle()
                did(dve.tensor_scalar(tile_i[:], rank_i[:], 7, None, ALU.arith_shift_right))
                did(dve.tensor_scalar(slot_i[:], rank_i[:], P - 1, None, ALU.bitwise_and))
                settle()
                did(dve.tensor_copy(slot_f[:], slot_i[:]))
                did(dve.scalar_tensor_tensor(col_f[:], code[:], -float(TPE), tile_i[:], ALU.mult, ALU.add))
                settle()
                for k in range(TOPK):
                    for u in range(U):
                        dve.tensor_scalar(hot_s[:, k * U + u, :], iota_s[:], slot_f[:, k, u:u + 1], None, ALU.is_equal)
                        m = dve.tensor_scalar(hot_c[:, k * U + u, :], iota_c[:], col_f[:, k, u:u + 1],
                                              tok1[:, bass.ds(q * U + u, 1)], ALU.is_equal, ALU.mult)
                m.then_inc(hot_s_done, 1)

            def route_add(q):
                dve.wait_ge(ids_ps, q + 1)
                dve.tensor_tensor(ids[:], ids[:], ps[:, MB, 384:512], ALU.add).then_inc(ids_s, 1)

            did(dve.memset(v_ext[:], 0.0))
            did(dve.memset(ids[:], 0.0))
            did(dve.memset(run[:], 0.0))
            settle()
            did(dve.memset(v_ext[:, :, HD:HD + 1], 1.0))
            dve.wait_ge(x_in[0], 16)
            ln1_stats(0)
            dve.wait_ge(bias_ps, 1)
            did(dve.tensor_copy(bias_cols[:], ps[:, PT, 0:NBR]))
            dve.wait_ge(bcast_in, 48)
            dve.wait_ge(consts, 1)
            settle()
            normalise(0, 0)
            copy_qk(0)
            copy_v(0)
            normalise(1, 0)
            for c in range(DC):
                row_max(0, c)
            copy_qk(1)
            first_steps = step[0]
            counts = []

            def counted(q, last):
                body(q, last)
                counts.append(step[0])
            groups(dve, counted)
            assert counts[1] == PER_GROUP, counts
            for part in (route_softmax, route_choose, route_ranks, route_place, route_add):
                part(NU - 1)

            dve.wait_ge(ids_s, NU)
            dve.wait_ge(pick_s, NU)
            dve.tensor_copy(cnt_f[:], run[:]).then_inc(run_s, 1)
            dve.wait_ge(cnt_ps, 1)
            dve.wait_ge(run_s, 1)
            did(dve.tensor_scalar(cnt_f[:], ps[:, PT + 1, 0:NE], float(ITEM - 1), None, ALU.add))
            settle()
            did(dve.tensor_copy(cnt_i[:], cnt_f[:]))
            settle()
            did(dve.tensor_scalar(cnt_i[:], cnt_i[:], ITEM.bit_length() - 1, None, ALU.arith_shift_right))
            settle()
            did(dve.tensor_scalar(items[:], cnt_i[:], 1.0, None, ALU.max))
            did(dve.tensor_scalar(ids_get[:], ids[:], -1.0, 0.0, ALU.add, ALU.max))
            did(dve.tensor_scalar(ids_f[:], ids[:], 0.0, float(SKIP), ALU.is_equal, ALU.mult))
            settle()
            did(dve.scalar_tensor_tensor(ids_put[:], ids[:], -1.0, ids_f[:], ALU.add, ALU.add))
            settle()
            dve.memset(cw_now[:], 0.0).then_inc(lists, 1)

            g = dve.alloc_register("dve_item")
            dve.reg_mov(g, 1)

            def take_item(k):
                dve.wait_ge(xt_ps, k)
                for half in range(2):
                    dve.tensor_copy(cw_next[:, half, :], rows[half][:, D:ROW])
                dve.tensor_copy(xT[:], ps[:, OB, :].rearrange("p (c n) -> p c n", c=DC)).then_inc(xt_sb, 1)

            dve.wait_ge(lists, 1)
            dve.memset(cw_next[:], 0.0).then_inc(xt_sb, 1)
            dve.memset(cw_now[:], 0.0).then_inc(y_s, 2)
            dve.wait_ge(xt_sb, 1)
            take_item(1)
            with dve.Fori(0, NE) as e:
                n = dve.value_load(items[0:1, bass.ds(e, 1)], min_val=1, max_val=N // ITEM)
                with dve.Fori(0, n) as _i:
                    k = dve.snap(g)
                    dve.wait_ge(xt_sb, k + 1)
                    dve.wait_ge(y_s, k + 1)
                    dve.tensor_copy(cw_now[:], cw_next[:]).then_inc(cw_moved, 1)
                    dve.wait_ge(cw_moved, k)
                    take_item(k + 1)
                    dve.wait_ge(y_ps, k)
                    for half in range(2):
                        m = dve.tensor_tensor(yb[:, half, :], ps[:, PT + half, 0:D],
                                              b2_bc[:, bass.ds(e, 1), :].rearrange("p o d -> p (o d)"), ALU.add)
                    m.then_inc(y_b, 1)
                    dve.wait_ge(y_b, k)
                    dve.wait_ge(put_s, (k + 2) * 32)
                    for half in range(2):
                        m = dve.tensor_scalar(yw[half][:], yb[:, half, :],
                                              cw_now[:, half, bass.ds(e, 1)], None, ALU.mult)
                    m.then_inc(y_s, 1)
                    dve.reg_add(g, g, 1)

        @block.gpsimd
        def _(pool):
            n = [0]

            def did(m):
                n[0] += 1
                m.then_inc(pool_step, 1)

            def settle():
                pool.wait_ge(pool_step, n[0])

            did(pool.memset(ident[:], 0.0))
            did(pool.memset(head_mask[:], SCALE))
            did(pool.memset(ones_bf[:], 1.0))
            did(pool.memset(minus_half[:], -0.5))
            did(pool.iota(iota_i[:], pattern=[[1, P]], base=0, channel_multiplier=0))
            did(pool.iota(codes_i[:], pattern=[[0, U], [-1, NE]], base=NE, channel_multiplier=0))
            did(pool.iota(tok_i[:], pattern=[[P, NB]], base=1, channel_multiplier=1))
            settle()
            did(pool.affine_select(out=ident[:], in_=ident[:], compare_op=ALU.not_equal, fill=1.0, base=0,
                                   pattern=[[-1, P]], channel_multiplier=1))
            did(pool.affine_select(out=earlier[:], in_=ones_bf[:], compare_op=ALU.is_gt, fill=0.0, base=0,
                                   pattern=[[1, P]], channel_multiplier=-1))
            did(pool.affine_select(out=head_mask[:], in_=head_mask[:], compare_op=ALU.is_ge, fill=0.0, base=0,
                                   pattern=[[-HD, HC]], channel_multiplier=1))
            did(pool.tensor_copy(iota_s[:], iota_i[:]))
            did(pool.tensor_copy(codes[:], codes_i[:]))
            did(pool.tensor_copy(tok1[:], tok_i[:]))
            settle()
            did(pool.tensor_scalar(iota_c[:], iota_s[:], -float(NE * TPE), None, ALU.add))
            did(pool.affine_select(out=head_mask[:], in_=head_mask[:], compare_op=ALU.is_ge, fill=0.0, base=HD - 1,
                                   pattern=[[HD, HC]], channel_multiplier=-1))
            settle()
            pool.memset(yw[0][:], 0.0).then_inc(consts, 1)

            def ln1_rstd(q):
                pool.wait_ge(stats_done, q + 1)
                pool.tensor_tensor(rstd[:, bass.ds(q * U, U)], vare[:, bass.ds(q * U, U)], minus_half[:, 0:U], ALU.pow
                                   ).then_inc(rstd_done, 1)

            def mask_keys(b):
                pool.wait_ge(qk_sb, b + 1)
                for c in range(DC):
                    pool.tensor_tensor(kmask[:, c, :, :], qkT[:, DC + c:DC + c + 1, :].to_broadcast([P, HC, P]),
                                       head_mask[:].unsqueeze(2).to_broadcast([P, HC, P]), ALU.mult
                                       ).then_inc(kmask_s, 1)

            def body(q, last):
                if not last:
                    ln1_rstd(q + 1)
                for u in range(U):
                    b = q * U + u
                    pool.wait_ge(var2_s, b + 1)
                    pool.tensor_tensor(rstd2[:], vare2[:], minus_half[:, 0:1], ALU.pow).then_inc(rstd2_s, 1)
                    if not (last and u >= U - 2):
                        pool.wait_ge(s_ps, (b + 2) * DC)
                        mask_keys(b + 2)

            def add_rows():
                for half in range(2):
                    pool.indirect_dma_start(out_rows, bass.IndirectOffsetOnAxis(put_idx[:, half:half + 1], 0),
                                            yw[half][:], None, bounds_check=N - 1, oob_is_err=False,
                                            compute_op=ALU.add).then_inc(put_s, 16)

            for rows_of in (put_idx, put_next, put_new):
                pool.memset(rows_of[:], SKIP).then_inc(put_q, 1)
            pool.memset(yw[1][:], 0.0).then_inc(pool_step, 1)
            ln1_rstd(0)
            mask_keys(0)
            pool.wait_ge(s_ps, DC)
            mask_keys(1)
            pool.wait_ge(put_q, 3)
            pool.wait_ge(pool_step, n[0] + 1)
            pool.wait_ge(consts, 1)
            add_rows()
            groups(pool, body)

            pool.wait_ge(lists, 1)
            pool.wait_ge(xn2_out, NB * 16)
            pool.wait_ge(cw_out, NU * 16)
            pool.wait_ge(x1_out, NB * 16)
            g = pool.alloc_register("pool_item")
            pool.reg_mov(g, 1)

            def get_rows():
                for half in range(2):
                    pool.indirect_dma_start(rows[half][:], None, table,
                                            bass.IndirectOffsetOnAxis(get_idx[:, half:half + 1], 0)
                                            ).then_inc(gat, 16)

            def put_rows(k, col):
                wait_alone(pool, put_s, k * 32)
                wait_alone(pool, put_q, k * 3)
                pool.tensor_copy(put_idx[:], put_next[:]).then_inc(put_q, 1)
                wait_alone(pool, put_q, k * 3 + 1)
                pool.tensor_copy(put_next[:], put_new[:]).then_inc(put_q, 1)
                wait_alone(pool, put_q, k * 3 + 2)
                pool.tensor_copy(put_new[:], ids_put[:, bass.ds(col, 2)]).then_inc(put_q, 1)
                wait_alone(pool, y_s, k)
                add_rows()

            with pool.Fori(0, NE) as e:
                m = pool.value_load(items[0:1, bass.ds(e, 1)], min_val=1, max_val=N // ITEM)
                with pool.Fori(0, m) as i:
                    k = pool.snap(g)
                    col = e * TPE + i * 2
                    wait_alone(pool, xt_sb, k)
                    pool.tensor_copy(get_idx[:], ids_get[:, bass.ds(col, 2)]).then_inc(idx_s, 1)
                    wait_alone(pool, idx_s, k)
                    get_rows()
                    put_rows(k, col)
                    pool.reg_add(g, g, 1)
            k = pool.snap(g)
            wait_alone(pool, xt_sb, k)
            get_rows()
            put_rows(k, 0)
            put_rows(k + 1, 0)
            wait_alone(pool, gat, k * 32)


_INS = ["x", "ctx_1024", "L0_xattn_wq", "L0_xattn_bq", "L0_xattn_wk", "L0_xattn_bk", "L0_xattn_wv", "L0_xattn_bv",
        "L0_ffn_Wg", "L0_ffn_bg", "L0_ffn_W1", "L0_ffn_b1", "L0_ffn_W2", "L0_ffn_b2"]


def kernel(**inputs):
    import numpy as _np
    import concourse.bacc as _bacc
    from concourse import mybir as _mybir
    from concourse.bass_utils import run_bass_kernel_spmd as _run

    nc = _bacc.Bacc("TRN2", target_bir_lowering=False, num_devices=1)
    arrays, args = {}, []
    for name in _INS:
        a = _np.ascontiguousarray(inputs[name])
        arrays[f"in_{name}"] = a
        args.append(nc.dram_tensor(f"in_{name}", a.shape, _mybir.dt.from_np(a.dtype), kind="ExternalInput").ap())
    shape = arrays["in_x"].shape
    args.append(nc.dram_tensor("out_0", shape, _mybir.dt.float32, kind="ExternalOutput").ap())
    build_xattn_moe(nc, *args)
    r = _run(nc, [arrays], core_ids=[0])
    return r.results[0]["out_0"]
```

```python
from contextlib import ExitStack

import concourse.bass as bass
from concourse import mybir

P = 128
ALU = mybir.AluOpType
ACT = mybir.ActivationFunctionType
AX_X = mybir.AxisListType.X
F32 = mybir.dt.float32
F32R = mybir.dt.float32r
F16 = mybir.dt.float16
BF16 = mybir.dt.bfloat16
I32 = mybir.dt.int32


def build_xattn_moe(nc, x, ctx_in, wq, bq, wk, bk, wv, bv, wg, bg, w1, b1, w2, b2, out):
    NB, S, D = x.shape
    NE, _, F = w1.shape
    HEADS = 16
    HD = D // HEADS
    DC = D // P
    FC = F // P
    HC = HEADS // DC
    GH = 4
    NG = HEADS // GH
    VW = 32
    U = 4
    NU = NB // U
    N = NB * S
    TPE = N // P
    ITEM = 2 * P
    ROW = D + NE
    SKIP = 2 * N
    SCALE = 1.0 / HD ** 0.5
    TOPK = 2
    assert S == P and NU >= 2 and NE == 8

    x_v = x.rearrange("b s d -> s b d")
    out_v = out
    out_rows = out.rearrange("b s d -> (b s) d")
    w1_v = w1.rearrange("e (c p) f -> e p c f", p=P)
    w2_v = w2.rearrange("e (c p) d -> e p c d", p=P)
    table = nc.dram_tensor("token_table", [N, ROW], F32).ap()
    table_v = table.rearrange("(b s) d -> b s d", s=S)

    with ExitStack() as stack:
        def sb(name, shape, dt=F32):
            return stack.enter_context(nc.sbuf_tensor(name, shape, dt))

        def sem(name):
            return stack.enter_context(nc.semaphore(name))

        ident = sb("ident", [P, P])
        head_mask = sb("head_mask", [P, HC])
        earlier = sb("earlier", [P, P], BF16)
        ones_bf = sb("ones_bf", [P, P], BF16)
        iota_s = sb("iota_s", [P, P])
        iota_c = sb("iota_c", [P, P])
        codes = sb("codes", [P, U, NE])
        iota_i = sb("iota_i", [P, P], I32)
        codes_i = sb("codes_i", [P, U, NE], I32)
        tok_i = sb("tok_i", [P, NB], I32)
        tok1 = sb("tok1", [P, NB])
        minus_half = sb("minus_half", [P, NB])
        wq_sb = sb("wq_sb", [P, DC, D])
        wk_sb = sb("wk_sb", [P, DC, D])
        wv_sb = sb("wv_sb", [P, DC, D])
        wg_sb = sb("wg_sb", [P, DC, NE])
        bv_bc = sb("bv_bc", [P, D])
        bg_bc = sb("bg_bc", [P, NE])
        b2_bc = sb("b2_bc", [P, NE, D])
        NBR = NE * FC + 2 * DC
        bias_rows = sb("bias_rows", [NBR, P])
        bias_cols = sb("bias_cols", [P, NBR])

        x_all = sb("x_all", [P, NB, D])
        ctx_sb = sb("ctx_sb", [P, D])
        stats = sb("stats", [P, U, 6])
        mv = sb("mv", [P, U, 2])
        mean = sb("mean", [P, NB])
        rstd = sb("rstd", [P, NB])
        vare = sb("vare", [P, NB])
        xn = sb("xn", [P, D])
        xcT = sb("xcT", [P, 2 * DC, P])
        qkT = sb("qkT", [P, 2 * DC, P])
        kmask = sb("kmask", [P, DC, HC, P])
        v_ext = sb("v_ext", [P, HEADS, VW])
        negmax = sb("negmax", [P, HEADS])
        probs = sb("probs", [P, HEADS, P])
        pT = sb("pT", [P, 2, GH, P])
        oT_sb = sb("oT_sb", [P, NG, P])
        inv_sum = sb("inv_sum", [P, HEADS])
        att = sb("att", [P, D])
        x1 = sb("x1", [P, D])
        stats2 = sb("stats2", [P, 6])
        mv2 = sb("mv2", [P, 2])
        vare2 = sb("vare2", [P, 1])
        rstd2 = sb("rstd2", [P, 1])
        xn2 = sb("xn2", [P, D])
        xn2T = sb("xn2T", [P, DC, P])
        lg = sb("lg", [P, U, NE])
        lgs = sb("lgs", [P, U, NE])
        ex = sb("ex", [P, U, NE])
        lgm = sb("lgm", [P, U, NE])
        eq = sb("eq", [P, U, NE])
        biggest = sb("biggest", [P, TOPK, U])
        ex_sum = sb("ex_sum", [P, U])
        den = sb("den", [P, U])
        inv_den = sb("inv_den", [P, U])
        top = sb("top", [P, TOPK, U])
        code = sb("code", [P, TOPK, U])
        onehot = sb("onehot", [P, TOPK, U, NE])
        ohr = sb("ohr", [P, TOPK, U, NE])
        oht = sb("oht", [P, TOPK, U, NE])
        ohw = sb("ohw", [P, TOPK, U, NE])
        wtop = sb("wtop", [P, TOPK, U])
        cw = sb("cw", [P, U, NE])
        picked = sb("picked", [P, U, NE], BF16)
        run = sb("run", [P, NE], BF16)
        picks = sb("picks", [P, NE], BF16)
        pick_sums = sb("pick_sums", [P, 2, NE], BF16)
        rank = sb("rank", [P, TOPK, U])
        rank_i = sb("rank_i", [P, TOPK, U], I32)
        tile_i = sb("tile_i", [P, TOPK, U], I32)
        slot_i = sb("slot_i", [P, TOPK, U], I32)
        slot_f = sb("slot_f", [P, TOPK, U])
        col_f = sb("col_f", [P, TOPK, U])
        hot_s = sb("hot_s", [P, TOPK * U, P], F16)
        hot_c = sb("hot_c", [P, TOPK * U, P], F16)
        ids = sb("ids", [P, NE * TPE])
        ids_f = sb("ids_f", [P, NE * TPE])
        ids_get = sb("ids_get", [P, NE * TPE], I32)
        ids_put = sb("ids_put", [P, NE * TPE], I32)
        cnt_f = sb("cnt_f", [P, NE])
        cnt_i = sb("cnt_i", [P, NE], I32)
        items = sb("items", [P, NE], I32)
        more_items = sb("more_items", [P, NE], I32)
        w1_raw = [sb(f"w1_raw{i}", [P, DC, F]) for i in range(2)]
        w2_raw = [sb(f"w2_raw{i}", [P, FC, D]) for i in range(2)]
        w1_hi = [sb(f"w1_hi{i}", [P, DC, F], F32R) for i in range(2)]
        w2_hi = [sb(f"w2_hi{i}", [P, FC, D], F32R) for i in range(2)]
        w1_lo = [sb(f"w1_lo{i}", [P, DC, F], F32R) for i in range(2)]
        w2_lo = [sb(f"w2_lo{i}", [P, FC, D], F32R) for i in range(2)]
        get_idx = sb("get_idx", [P, 2], I32)
        put_new = sb("put_new", [P, 2], I32)
        put_next = sb("put_next", [P, 2], I32)
        put_idx = sb("put_idx", [P, 2], I32)
        rows0 = sb("rows0", [P, ROW])
        rows1 = sb("rows1", [P, ROW])
        rows = [rows0, rows1]
        cw_next = sb("cw_next", [P, 2, NE])
        cw_now = sb("cw_now", [P, 2, NE])
        xT_hi = sb("xT_hi", [P, DC, ITEM], F32R)
        xT_lo = sb("xT_lo", [P, DC, ITEM], F32R)
        bias_now = [sb(f"bias_now{i}", [P, FC]) for i in range(2)]
        h_chunk = sb("h_chunk", [P, 4, ITEM])
        hT_hi = sb("hT_hi", [P, FC, ITEM], F32R)
        hT_lo = sb("hT_lo", [P, FC, ITEM], F32R)
        yb = sb("yb", [P, 2, D])
        yw0 = sb("yw0", [P, D])
        yw1 = sb("yw1", [P, D])
        yw = [yw0, yw1]

        ps = stack.enter_context(nc.psum_tensor("ps", [P, 8, 512], F32))
        PT, OB, MB = 4, 6, 7
        RK = D

        x_in = [sem("x_in_first"), sem("x_in_rest")]
        ctx_s = sem("ctx_loaded")
        wts_in = sem("attn_weights_loaded")
        small_in = sem("bias_rows_loaded")
        bcast_in = sem("broadcast_biases_loaded")
        consts = sem("constants_built")
        pool_step = sem("pool_step")
        bias_ps = sem("biases_transposed")
        dve_step = sem("dve_step")
        stats_done = sem("ln1_stats_done")
        rstd_done = sem("ln1_rstd_done")
        xn_done = sem("xn_done")
        xcT_ps = sem("xcT_in_psum")
        xcT_sb = sem("xcT_in_sbuf")
        qk_ps = sem("qk_in_psum")
        qk_sb = sem("qk_in_sbuf")
        v_ps = sem("v_in_psum")
        v_sb = sem("v_in_sbuf")
        kmask_s = sem("kmask_done")
        s_ps = sem("scores_in_psum")
        max_s = sem("negmax_done")
        exp_s = sem("probs_done")
        pT_ps = sem("pT_in_psum")
        pT_dve = sem("pT_copied_by_dve")
        pT_act = sem("pT_copied_by_act")
        pv_s = sem("pv_in_psum")
        o_sb = sem("oT_in_sbuf")
        o_ps = sem("o_in_psum")
        x1_s = sem("x1_done")
        x1_out = sem("x1_stored")
        var2_s = sem("ln2_var_done")
        rstd2_s = sem("ln2_rstd_done")
        xn2_s = sem("xn2_done")
        xn2_out = sem("xn2_stored")
        xn2T_ps = sem("xn2T_in_psum")
        xn2T_sb = sem("xn2T_in_sbuf")
        lg_ps = sem("logits_in_psum")
        lg_read = sem("logits_read")
        lg_s = sem("logits_shifted")
        ex_s = sem("router_exp_done")
        cw_s = sem("combine_weights_done")
        cw_out = sem("combine_weights_stored")
        pick_s = sem("choices_done")
        rank_read = sem("ranks_read")
        rank_ps = sem("ranks_in_psum")
        hot_s_done = sem("onehots_done")
        ids_ps = sem("ids_in_psum")
        ids_s = sem("ids_added")
        run_s = sem("totals_done")
        cnt_ps = sem("counts_in_psum")
        lists = sem("lists_ready")
        w_in = [sem("ffn_weights0_loaded"), sem("ffn_weights1_loaded")]
        idx_s = sem("gather_indices_copied")
        gat = sem("rows_gathered")
        xt_ps = sem("item_transposed")
        xt_sb = sem("item_in_sbuf")
        h_ps = sem("hidden_in_psum")
        h_act = sem("hidden_gelu_done")
        hi_done = sem("weights_high_parts_done")
        lo1_done = sem("w1_low_part_done")
        lo2_done = sem("w2_low_part_done")
        bias_s = sem("expert_bias_copied")
        xt_hi = sem("item_high_part_done")
        h_hi = sem("hidden_high_parts_done")
        h_sb = sem("hidden_pairs_split")
        y_ps = sem("y_in_psum")
        y_b = sem("y_biased")
        y_s = sem("y_scaled")
        cw_moved = sem("cw_moved")
        put_s = sem("rows_added")
        put_q = sem("put_queue_moved")

        block = stack.enter_context(nc.Block())

        wait_registers = {}

        def wait_alone(eng, signal, value):
            if not isinstance(value, int):
                if eng.engine not in wait_registers:
                    wait_registers[eng.engine] = eng.alloc_register(f"wait_value_{len(wait_registers)}")
                eng.reg_mov(wait_registers[eng.engine], value)
                value = wait_registers[eng.engine]
            eng.wait_ge(consts, 1)
            eng.wait_ge(signal, value)

        def groups(eng, body):
            body(0, False)
            with eng.Fori(1, NU - 1) as q:
                body(q, False)
            body(NU - 1, True)

        @block.sync
        def _(sp):
            sp.dma_start(x_all[:, 0:U, :], x_v[:, 0:U, :]).then_inc(x_in[0], 16)
            sp.dma_start(ctx_sb[:], ctx_in[0]).then_inc(ctx_s, 16)
            sp.dma_start(x_all[:, U:, :], x_v[:, U:, :]).then_inc(x_in[1], 16)
            for b in range(2):
                sp.wait_ge(xcT_ps, b + 1)
                sp.dma_start(ctx_sb[:], ctx_in[b + 1]).then_inc(ctx_s, 16)

            def store_cw(q):
                sp.wait_ge(cw_s, q + 1)
                sp.dma_start(table_v[bass.ds(q * U, U), :, D:ROW].rearrange("b s e -> s b e"),
                             cw[:]).then_inc(cw_out, 16)

            def body(q, last):
                for u in range(U):
                    b = q * U + u
                    sp.wait_ge(x1_s, b + 1)
                    sp.dma_start(out_v[bass.ds(b, 1)].rearrange("o s d -> (o s) d"), x1[:]).then_inc(x1_out, 16)
                    sp.wait_ge(xn2_s, b + 1)
                    sp.dma_start(table_v[bass.ds(b, 1), :, 0:D].rearrange("o s d -> (o s) d"),
                                 xn2[:]).then_inc(xn2_out, 16)
                    if not (last and u >= U - 3):
                        sp.wait_ge(xcT_ps, b + 3)
                        sp.dma_start(ctx_sb[:], ctx_in[bass.ds(b + 3, 1)].rearrange("o s d -> (o s) d")
                                     ).then_inc(ctx_s, 16)
                    if u == 3 and not (isinstance(q, int) and q == 0):
                        store_cw(q - 1)
            groups(sp, body)
            store_cw(NU - 1)

            sp.wait_ge(x1_out, NB * 16)
            sp.wait_ge(xn2_out, NB * 16)
            sp.wait_ge(cw_out, (NU + 1) * 16)
            with sp.Fori(0, NE // 2 - 1) as pair:
                for par in range(2):
                    sp.wait_ge(lo1_done, pair * 2 + (par + 1))
                    sp.wait_ge(lo2_done, pair * 2 + (par + 1))
                    e = pair * 2 + (par + 2)
                    sp.dma_start(w1_raw[par][:], w1_v[bass.ds(e, 1)].rearrange("o p c f -> (o p) c f")
                                 ).then_inc(w_in[par], 16)
                    sp.dma_start(w2_raw[par][:], w2_v[bass.ds(e, 1)].rearrange("o p c d -> (o p) c d")
                                 ).then_inc(w_in[par], 16)
            sp.wait_ge(lists, 1)
            done = sp.alloc_register("sp_items_done")
            sp.reg_mov(done, 0)
            for e in range(NE):
                n = sp.value_load(items[0:1, e:e + 1], min_val=2, max_val=N // ITEM)
                sp.reg_add(done, done, n)
            total = sp.snap(done)
            wait_alone(sp, put_s, (total + 3) * 32)

        @block.tensor
        def _(pe):
            def rank_group(q):
                pe.wait_ge(pick_s, q + 1)
                rk = ps[:, MB, RK:RK + U * NE]
                pk = picked[:].rearrange("p u e -> p (u e)")
                pe.matmul(rk, earlier[:], pk, start=True, stop=False)
                for d in range(1, U):
                    pe.matmul(rk[:, d * NE:], ones_bf[:], pk[:, :(U - d) * NE], start=False, stop=False)
                for u in range(U):
                    m = pe.matmul(rk[:, u * NE:(u + 1) * NE], ones_bf[:], run[:], start=False, stop=(u == U - 1))
                m.then_inc(rank_ps, 1)

            def place_ids(q):
                pe.wait_ge(hot_s_done, q + 1)
                for k in range(TOPK * U):
                    m = pe.matmul(ps[:, MB, 384:512], hot_s[:, k, :], hot_c[:, k, :],
                                  start=(k == 0), stop=(k == TOPK * U - 1))
                m.then_inc(ids_ps, 1)

            def prep(b):
                pe.wait_ge(consts, 1)
                pe.wait_ge(xn_done, b + 1)
                pe.wait_ge(ctx_s, (b + 1) * 16)
                if isinstance(b, int) and b == 0:
                    pass
                else:
                    pe.wait_ge(v_sb, b)
                for j in range(2 * DC):
                    src = xn if j < DC else ctx_sb
                    m = pe.transpose(ps[:, MB, j * P:(j + 1) * P], src[:, (j % DC) * P:(j % DC + 1) * P], ident[:])
                m.then_inc(xcT_ps, 1)
                pe.wait_ge(xcT_sb, b + 1)
                if isinstance(b, int) and b == 0:
                    pe.wait_ge(wts_in, 64)
                for j in range(2 * DC):
                    w = wq_sb if j < DC else wk_sb
                    src = 0 if j < DC else DC
                    for c in range(DC):
                        m = pe.matmul(ps[:, OB, j * P:(j + 1) * P], w[:, c, (j % DC) * P:(j % DC + 1) * P],
                                      xcT[:, src + c, :], start=(c == 0), stop=(c == DC - 1))
                m.then_inc(qk_ps, 1)
                for c in range(DC):
                    m = pe.matmul(ps[:, MB, 0:D], xcT[:, DC + c, :], wv_sb[:, c, :],
                                  start=(c == 0), stop=(c == DC - 1))
                m.then_inc(v_ps, 1)

            def scores(b):
                pe.wait_ge(qk_sb, b + 1)
                for c in range(DC):
                    pe.wait_ge(kmask_s, b * DC + c + 1)
                    for g in range(HC // GH):
                        m = pe.matmul(ps[:, c * (HC // GH) + g, :], qkT[:, c, :],
                                      kmask[:, c, g * GH:(g + 1) * GH, :], start=True, stop=True)
                    m.then_inc(s_ps, 1)

            def turn_probs(b, g):
                pe.wait_ge(exp_s, b * NG + g + 1)
                if g >= 2:
                    pe.wait_ge(pT_act if g % 2 else pT_dve, b * (NG // 2) + g // 2)
                elif g == 1 and not (isinstance(b, int) and b == 0):
                    pe.wait_ge(lg_read, b)
                for i in range(GH):
                    m = pe.transpose(ps[:, PT + g % 2, i * P:(i + 1) * P], probs[:, g * GH + i, :], ident[:])
                m.then_inc(pT_ps, 1)

            def times_v(b, g, more1):
                pe.wait_ge(pT_act if g % 2 else pT_dve, b * (NG // 2) + g // 2 + 1)
                if g == 0:
                    pe.wait_ge(v_sb, b + 1)
                    if more1:
                        pe.wait_ge(qk_sb, b + 2)
                for i in range(GH):
                    m = pe.matmul(ps[i * VW:(i + 1) * VW, OB, g * P:(g + 1) * P],
                                  v_ext[:, g * GH + i, :], pT[:, g % 2, i, :], start=True, stop=True,
                                  tile_position=(0, i * VW))
                m.then_inc(pv_s, 1)

            def body(q, last):
                for u in range(U):
                    b = q * U + u
                    more1 = not (last and u >= U - 1)
                    more2 = not (last and u >= U - 2)
                    turn_probs(b, 0)
                    turn_probs(b, 1)
                    for g in range(NG):
                        times_v(b, g, more1)
                        if g + 2 < NG:
                            turn_probs(b, g + 2)
                    if more1:
                        scores(b + 1)
                    pe.wait_ge(o_sb, b + 1)
                    for g in range(NG):
                        m = pe.transpose(ps[:, PT, g * P:(g + 1) * P], oT_sb[:, g, :], ident[:])
                    m.then_inc(o_ps, 1)
                    if more2:
                        if u == 2 and not (isinstance(q, int) and q == 0):
                            pe.wait_ge(rank_read, q)
                        if u == 0 and not (isinstance(q, int) and q == 0):
                            pe.wait_ge(ids_s, q)
                        prep(b + 2)
                    pe.wait_ge(xn2_s, b + 1)
                    for c in range(DC):
                        m = pe.transpose(ps[:, PT + 1, c * P:(c + 1) * P], xn2[:, c * P:(c + 1) * P], ident[:])
                    m.then_inc(xn2T_ps, 1)
                    pe.wait_ge(xn2T_sb, b + 1)
                    for c in range(DC):
                        m = pe.matmul(ps[:, PT + 1, D + u * NE:D + (u + 1) * NE], xn2T[:, c, :], wg_sb[:, c, :],
                                      start=(c == 0), stop=(c == DC - 1))
                    m.then_inc(lg_ps, 1)
                    if u == 1 and not (isinstance(q, int) and q == 0):
                        rank_group(q - 1)
                    if u == 3 and not (isinstance(q, int) and q == 0):
                        place_ids(q - 1)

            pe.wait_ge(consts, 1)
            pe.wait_ge(small_in, 48)
            pe.transpose(ps[:, PT, 0:NBR], bias_rows[:], ident[0:NBR, 0:NBR]).then_inc(bias_ps, 1)
            prep(0)
            scores(0)
            prep(1)
            groups(pe, body)
            rank_group(NU - 1)
            pe.wait_ge(ids_s, NU)
            place_ids(NU - 1)
            pe.wait_ge(run_s, 1)
            pe.matmul(ps[:, PT + 1, 0:NE], ones_bf[:], picks[:], start=True, stop=True).then_inc(cnt_ps, 1)

            g = pe.alloc_register("pe_item")
            pe.reg_mov(g, 1)
            chunks = pe.alloc_register("pe_chunks")
            pe.reg_mov(chunks, 0)
            pairs = pe.alloc_register("pe_pairs")
            pe.reg_mov(pairs, 0)

            def turn_item(k):
                pe.wait_ge(gat, k * 32)
                pe.wait_ge(xt_sb, k)
                for half in range(2):
                    for c in range(DC):
                        m = pe.transpose(ps[:, OB, c * ITEM + half * P:c * ITEM + (half + 1) * P],
                                         rows[half][:, c * P:(c + 1) * P], ident[:])
                m.then_inc(xt_ps, 1)

            pe.wait_ge(lists, 1)
            turn_item(1)
            with pe.Fori(0, NE // 2) as pair:
                for par in range(2):
                    n = pe.value_load(items[0:1, bass.ds(pair * 2 + par, 1)], min_val=2, max_val=N // ITEM)
                    wait_alone(pe, lo1_done, pair * 2 + (par + 1))
                    with pe.Fori(0, n) as _i:
                        k = pe.snap(g)
                        hc = pe.snap(chunks)
                        hp = pe.snap(pairs)
                        pe.wait_ge(xt_sb, k + 1)
                        for f in range(FC):
                            if f >= 4:
                                pe.wait_ge(h_act, hc + f - 3)
                            for c in range(DC):
                                w_hi = w1_hi[par][:, c, f * P:(f + 1) * P]
                                w_lo = w1_lo[par][:, c, f * P:(f + 1) * P]
                                hidden = ps[:, f % 4, 0:ITEM]
                                pe.matmul(hidden, w_hi, xT_lo[:, c, :], start=(c == 0), stop=False)
                                pe.matmul(hidden, w_lo, xT_hi[:, c, :], start=False, stop=False)
                                m = pe.matmul(hidden, w_hi, xT_hi[:, c, :], start=False, stop=(c == DC - 1))
                            m.then_inc(h_ps, 1)
                        turn_item(k + 1)
                        pe.wait_ge(lo2_done, pair * 2 + (par + 1))
                        pe.wait_ge(y_s, k + 1)
                        for f in range(FC):
                            if f % 2 == 0:
                                pe.wait_ge(h_sb, hp + f // 2 + 3)
                            for half in range(2):
                                y = ps[:, PT + half, 0:D]
                                h_lo_f = hT_lo[:, f, half * P:(half + 1) * P]
                                h_hi_f = hT_hi[:, f, half * P:(half + 1) * P]
                                pe.matmul(y, h_lo_f, w2_hi[par][:, f, :], start=(f == 0), stop=False)
                                pe.matmul(y, h_hi_f, w2_lo[par][:, f, :], start=False, stop=False)
                                m = pe.matmul(y, h_hi_f, w2_hi[par][:, f, :], start=False, stop=(f == FC - 1))
                        m.then_inc(y_ps, 1)
                        pe.reg_add(g, g, 1)
                        pe.reg_add(chunks, chunks, FC)
                        pe.reg_add(pairs, pairs, FC // 2)

        @block.scalar
        def _(act):
            act.dma_start(bias_rows[0:NE * FC, :], b1.rearrange("e (f p) -> (e f) p", p=P)).then_inc(small_in, 16)
            act.dma_start(bias_rows[NE * FC:NE * FC + DC, :], bq.rearrange("(c p) -> c p", p=P)).then_inc(small_in, 16)
            act.dma_start(bias_rows[NE * FC + DC:NBR, :], bk.rearrange("(c p) -> c p", p=P)).then_inc(small_in, 16)
            act.dma_start(wq_sb[:], wq.rearrange("(c p) n -> p c n", p=P)).then_inc(wts_in, 16)
            act.dma_start(wk_sb[:], wk.rearrange("(c p) n -> p c n", p=P)).then_inc(wts_in, 16)
            act.dma_start(wv_sb[:], wv.rearrange("(c p) n -> p c n", p=P)).then_inc(wts_in, 16)
            act.dma_start(wg_sb[:], wg.rearrange("(c p) n -> p c n", p=P)).then_inc(wts_in, 16)
            act.dma_start(bv_bc[:], bv.partition_broadcast(P)).then_inc(bcast_in, 16)
            act.dma_start(bg_bc[:], bg.partition_broadcast(P)).then_inc(bcast_in, 16)
            act.dma_start(b2_bc[:], b2.partition_broadcast(P)).then_inc(bcast_in, 16)
            for par in range(2):
                act.dma_start(w1_raw[par][:], w1_v[par]).then_inc(w_in[par], 16)
                act.dma_start(w2_raw[par][:], w2_v[par]).then_inc(w_in[par], 16)

            def copy_xcT(b):
                act.wait_ge(xcT_ps, b + 1)
                act.copy(xcT[:], ps[:, MB, :].rearrange("p (j n) -> p j n", j=2 * DC)).then_inc(xcT_sb, 1)

            def router_exp(q):
                act.wait_ge(lg_s, q + 1)
                act.activation(ex[:], lgs[:], ACT.Exp).then_inc(ex_s, 1)

            def exp_probs(b, chunks=range(DC)):
                for c in chunks:
                    act.wait_ge(max_s, b * DC + c + 1)
                    for h in range(c * HC, (c + 1) * HC):
                        m = act.activation(probs[:, h, :], ps[:, h // GH, (h % GH) * P:(h % GH + 1) * P], ACT.Exp,
                                           bias=negmax[:, h:h + 1])
                        if h % GH == GH - 1:
                            m.then_inc(exp_s, 1)

            def body(q, last):
                for u in range(U):
                    b = q * U + u
                    for g in (1, 3):
                        act.wait_ge(pT_ps, b * NG + g + 1)
                        if g == 3:
                            act.wait_ge(pv_s, b * NG + 2)
                        act.copy(pT[:, 1, :, :], ps[:, PT + 1, :].rearrange("p (i n) -> p i n", i=GH)
                                 ).then_inc(pT_act, 1)
                    act.wait_ge(pv_s, (b + 1) * NG)
                    act.copy(oT_sb[:], ps[:, OB, :].rearrange("p (g n) -> p g n", g=NG)).then_inc(o_sb, 1)
                    if not (last and u >= U - 1):
                        exp_probs(b + 1, [0])
                    if not (last and u >= U - 2):
                        copy_xcT(b + 2)
                    if not (last and u >= U - 1):
                        exp_probs(b + 1, range(1, DC))
                    act.wait_ge(xn2T_ps, b + 1)
                    act.copy(xn2T[:], ps[:, PT + 1, 0:D].rearrange("p (c n) -> p c n", c=DC)).then_inc(xn2T_sb, 1)
                    if u == 0 and not (isinstance(q, int) and q == 0):
                        router_exp(q - 1)

            copy_xcT(0)
            exp_probs(0)
            copy_xcT(1)
            groups(act, body)
            router_exp(NU - 1)

            g = act.alloc_register("act_chunks")
            act.reg_mov(g, 0)

            def round_weights(par, loads):
                act.wait_ge(w_in[par], loads)
                act.copy(w1_hi[par][:], w1_raw[par][:])
                act.copy(w2_hi[par][:], w2_raw[par][:]).then_inc(hi_done, 1)

            def gelu_item(par):
                k = act.snap(g)
                for f in range(FC):
                    act.wait_ge(h_ps, k + f + 1)
                    if f % 2 == 0:
                        act.wait_ge(h_sb, act.snap(p) + f // 2 + 1)
                    act.activation(h_chunk[:, f % 4, :], ps[:, f % 4, 0:ITEM], ACT.Gelu_apprx_tanh,
                                   bias=bias_now[par][:, f:f + 1]).then_inc(h_act, 1)
                act.reg_add(g, g, FC)
                act.reg_add(p, p, FC // 2)

            def expert(e, pair, par, last):
                n = act.value_load(more_items[0:1, bass.ds(e, 1)], min_val=1, max_val=N // ITEM - 1)
                act.copy(bias_now[par][:], bias_cols[:, bass.ds(e * FC, FC)]).then_inc(bias_s, 1)
                act.wait_ge(bias_s, e + 1)
                gelu_item(par)
                if not last:
                    round_weights(1 - par, (pair + par + 1) * 32)
                with act.Fori(0, n) as _i:
                    gelu_item(par)

            p = act.alloc_register("act_pairs")
            act.reg_mov(p, 0)
            round_weights(0, 32)
            act.wait_ge(lists, 1)
            with act.Fori(0, NE // 2 - 1) as pair:
                for par in range(2):
                    expert(pair * 2 + par, pair, par, False)
            for par in range(2):
                expert(NE - 2 + par, NE // 2 - 1, par, par == 1)

        @block.vector
        def _(dve):
            ROUTE_STEPS = 31
            PER_GROUP = 2 * U + 1 + 4 * U + ROUTE_STEPS
            step = [0]
            base = [0]

            def did(m):
                step[0] += 1
                m.then_inc(dve_step, 1)

            def settle(own=False):
                if own:
                    wait_alone(dve, dve_step, base[0] + step[0])
                else:
                    dve.wait_ge(dve_step, base[0] + step[0])

            def ln1_stats(q):
                for u in range(U):
                    did(dve.bn_stats(stats[:, u, :],
                                     x_all[:, bass.ds(q * U + u, 1), :].rearrange("p o d -> p (o d)")))
                settle(own=True)
                for u in range(U):
                    did(dve.bn_aggr(mv[:, u, :], stats[:, u, :]))
                settle()
                did(dve.tensor_copy(mean[:, bass.ds(q * U, U)], mv[:, :, 0:1].rearrange("p b o -> p (b o)")))
                dve.tensor_scalar(vare[:, bass.ds(q * U, U)], mv[:, :, 1:2].rearrange("p b o -> p (b o)"),
                                  1e-5, None, ALU.add).then_inc(stats_done, 1)

            def normalise(b, q):
                dve.wait_ge(rstd_done, q + 1)
                if isinstance(b, int) and b == 0:
                    pass
                else:
                    dve.wait_ge(xcT_ps, b)
                dve.tensor_scalar(xn[:], x_all[:, bass.ds(b, 1), :].rearrange("p o d -> p (o d)"),
                                  mean[:, bass.ds(b, 1)], rstd[:, bass.ds(b, 1)],
                                  ALU.subtract, ALU.mult).then_inc(xn_done, 1)

            def copy_qk(b):
                dve.wait_ge(qk_ps, b + 1)
                if not (isinstance(b, int) and b == 0):
                    dve.wait_ge(s_ps, b * DC)
                    dve.wait_ge(kmask_s, b * DC)
                dve.tensor_tensor(qkT[:], ps[:, OB, :].rearrange("p (j n) -> p j n", j=2 * DC),
                                  bias_cols[:, NE * FC:NBR].unsqueeze(2).to_broadcast([P, 2 * DC, P]),
                                  ALU.add).then_inc(qk_sb, 1)

            def copy_v(b):
                dve.wait_ge(v_ps, b + 1)
                if not (isinstance(b, int) and b == 0):
                    dve.wait_ge(pv_s, b * NG)
                dve.tensor_tensor(v_ext[:, :, 0:HD], ps[:, MB, 0:D].rearrange("p (h n) -> p h n", h=HEADS),
                                  bv_bc[:].rearrange("p (h n) -> p h n", h=HEADS), ALU.add).then_inc(v_sb, 1)

            def row_max(b, c):
                dve.wait_ge(s_ps, b * DC + c + 1)
                if c == 0 and not (isinstance(b, int) and b == 0):
                    dve.wait_ge(exp_s, b * NG)
                nb = HC // GH
                dve.tensor_reduce(negmax[:, c * HC:(c + 1) * HC],
                                  ps[:, c * nb:(c + 1) * nb, :].rearrange("p g (h n) -> p (g h) n", h=GH),
                                  AX_X, ALU.max, negate=True).then_inc(max_s, 1)

            def body(q, last):
                step[0] = 0
                base[0] = first_steps + (0 if isinstance(q, int) and q == 0 else q * PER_GROUP - ROUTE_STEPS)
                if not last:
                    dve.wait_ge(x_in[1], 16)
                    ln1_stats(q + 1)
                for u in range(U):
                    b = q * U + u
                    more1 = not (last and u >= U - 1)
                    more2 = not (last and u >= U - 2)
                    if more2:
                        normalise(b + 2, q if u < U - 2 else q + 1)
                    for g in (0, 2):
                        dve.wait_ge(pT_ps, b * NG + g + 1)
                        if g == 2:
                            dve.wait_ge(pv_s, b * NG + 1)
                        dve.tensor_copy(pT[:, 0, :, :], ps[:, PT, :].rearrange("p (i n) -> p i n", i=GH)
                                        ).then_inc(pT_dve, 1)
                        if not (isinstance(q, int) and q == 0):
                            route(q - 1, u, g // 2)
                    if more1:
                        copy_v(b + 1)
                    if not (isinstance(q, int) and q == 0):
                        route(q - 1, u, 2)
                    if more1:
                        for c in range(DC):
                            row_max(b + 1, c)
                    dve.wait_ge(o_ps, b + 1)
                    o_v = ps[:, PT, :].rearrange("p (h w) -> p h w", w=VW)
                    did(dve.reciprocal(inv_sum[:], o_v[:, :, HD:HD + 1].rearrange("p h o -> p (h o)")))
                    settle()
                    did(dve.tensor_tensor(att[:].rearrange("p (h n) -> p h n", h=HEADS), o_v[:, :, 0:HD],
                                          inv_sum[:].unsqueeze(2).to_broadcast([P, HEADS, HD]), ALU.mult))
                    settle()
                    if not (isinstance(q, int) and q == 0 and u == 0):
                        dve.wait_ge(x1_out, b * 16)
                    dve.tensor_tensor(x1[:], att[:], x_all[:, bass.ds(b, 1), :].rearrange("p o d -> p (o d)"),
                                      ALU.add).then_inc(x1_s, 1)
                    dve.wait_ge(x1_s, b + 1)
                    did(dve.bn_stats(stats2[:], x1[:]))
                    settle(own=True)
                    did(dve.bn_aggr(mv2[:], stats2[:]))
                    settle()
                    dve.tensor_scalar(vare2[:], mv2[:, 1:2], 1e-5, None, ALU.add).then_inc(var2_s, 1)
                    dve.wait_ge(rstd2_s, b + 1)
                    if not (isinstance(q, int) and q == 0 and u == 0):
                        dve.wait_ge(xn2_out, b * 16)
                    dve.tensor_scalar(xn2[:], x1[:], mv2[:, 0:1], rstd2[:], ALU.subtract, ALU.mult).then_inc(xn2_s, 1)
                    if more2:
                        copy_qk(b + 2)
                    if not (isinstance(q, int) and q == 0):
                        route(q - 1, u, 3)
                    dve.wait_ge(lg_ps, b + 1)
                    dve.tensor_tensor(lg[:, u, :], ps[:, PT + 1, D + u * NE:D + (u + 1) * NE], bg_bc[:], ALU.add
                                      ).then_inc(lg_read, 1)
                if not (isinstance(q, int) and q == 0):
                    route_add(q - 1)

            def bc(ap):
                return ap.unsqueeze(2).to_broadcast([P, U, NE])

            def experts(ap):
                return ap.rearrange("p k u -> p (k u)").unsqueeze(2).to_broadcast([P, TOPK * U, NE])

            def flat(ap):
                return ap.rearrange("p k u e -> p (k u) e")

            def route(q, u, place):
                if (u, place) == (0, 0):
                    dve.wait_ge(lg_read, (q + 1) * U)
                    largest(0, lg)
                    did(dve.tensor_tensor(eq[:], lg[:], bc(biggest[:, 0, :]), ALU.is_equal))
                    dve.tensor_tensor(lgs[:], lg[:], bc(biggest[:, 0, :]), ALU.subtract).then_inc(lg_s, 1)
                elif (u, place) == (0, 1):
                    first_of_equals(0)
                elif (u, place) == (0, 2):
                    did(dve.scalar_tensor_tensor(lgm[:], onehot[:, 0], -1e30, lg[:], ALU.mult, ALU.add))
                    settle()
                    largest(1, lgm)
                    dve.wait_ge(lg_s, q + 1)
                elif (u, place) == (0, 3):
                    did(dve.tensor_tensor(eq[:], lgm[:], bc(biggest[:, 1, :]), ALU.is_equal))
                    settle()
                elif (u, place) == (1, 0):
                    first_of_equals(1)
                elif (u, place) == (1, 1):
                    dve.wait_ge(rank_ps, q + 1)
                    did(dve.tensor_copy(run[:], picks[:]))
                    did(dve.tensor_tensor(picked[:], onehot[:, 0], onehot[:, 1], ALU.add))
                    settle()
                    did(dve.tensor_tensor(pick_sums[:, 0], picked[:, 0], picked[:, 1], ALU.add))
                    dve.tensor_tensor(pick_sums[:, 1], picked[:, 2], picked[:, 3], ALU.add).then_inc(pick_s, 1)
                    dve.wait_ge(pick_s, q + 1)
                elif (u, place) == (1, 2):
                    dve.wait_ge(ex_s, q + 1)
                    did(dve.tensor_reduce(ex_sum[:], ex[:], AX_X, ALU.add))
                    for k in range(TOPK):
                        did(dve.tensor_tensor(oht[:, k], onehot[:, k], ex[:], ALU.mult))
                    settle()
                elif (u, place) == (1, 3):
                    did(dve.tensor_reduce(top[:], oht[:], AX_X, ALU.add))
                    did(dve.tensor_tensor(pick_sums[:, 0], pick_sums[:, 0], pick_sums[:, 1], ALU.add))
                    settle()
                    did(dve.tensor_tensor(picks[:], run[:], pick_sums[:, 0], ALU.add))
                    did(dve.tensor_tensor(den[:], top[:, 0, :], top[:, 1, :], ALU.add))
                    settle()
                elif (u, place) == (2, 0):
                    did(dve.scalar_tensor_tensor(den[:], ex_sum[:], 1e-8, den[:], ALU.mult, ALU.add))
                    settle()
                    did(dve.reciprocal(inv_den[:], den[:]))
                    settle()
                elif (u, place) == (2, 1):
                    dve.wait_ge(rank_ps, q + 2)
                    rk = ps[:, MB, RK:RK + U * NE].rearrange("p (u e) -> p u e", u=U)
                    for k in range(TOPK):
                        m = dve.tensor_tensor(ohr[:, k], onehot[:, k], rk, ALU.mult)
                    m.then_inc(rank_read, 1)
                    did(dve.tensor_tensor(wtop[:], top[:], inv_den[:].unsqueeze(1).to_broadcast([P, TOPK, U]),
                                          ALU.mult))
                    dve.wait_ge(rank_read, q + 1)
                    settle()
                elif (u, place) == (2, 2):
                    did(dve.tensor_tensor(flat(ohw[:]), flat(onehot[:]), experts(wtop[:]), ALU.mult))
                    did(dve.tensor_reduce(rank[:], ohr[:], AX_X, ALU.add))
                    settle()
                    did(dve.tensor_copy(rank_i[:], rank[:]))
                elif (u, place) == (2, 3):
                    dve.wait_ge(cw_out, (q + 1) * 16)
                    dve.tensor_tensor(cw[:], ohw[:, 0], ohw[:, 1], ALU.add).then_inc(cw_s, 1)
                    settle()
                    did(dve.tensor_scalar(tile_i[:], rank_i[:], 7, None, ALU.arith_shift_right))
                    did(dve.tensor_scalar(slot_i[:], rank_i[:], P - 1, None, ALU.bitwise_and))
                    settle()
                elif (u, place) == (3, 0):
                    did(dve.tensor_copy(slot_f[:], slot_i[:]))
                    did(dve.scalar_tensor_tensor(col_f[:], code[:], -float(TPE), tile_i[:], ALU.mult, ALU.add))
                    settle()
                    one_hots(q, 0, 0, 2)
                elif (u, place) == (3, 1):
                    one_hots(q, 0, 2, U)
                elif (u, place) == (3, 2):
                    one_hots(q, 1, 0, 2)
                elif (u, place) == (3, 3):
                    one_hots(q, 1, 2, U).then_inc(hot_s_done, 1)

            def largest(k, values):
                did(dve.tensor_reduce(biggest[:, k, :], values[:], AX_X, ALU.max))
                settle()

            def first_of_equals(k):
                settle()
                did(dve.tensor_tensor(eq[:], eq[:], codes[:], ALU.mult))
                settle()
                did(dve.tensor_reduce(code[:, k, :], eq[:], AX_X, ALU.max))
                settle()
                did(dve.tensor_tensor(onehot[:, k], codes[:], bc(code[:, k, :]), ALU.is_equal))
                settle()

            def one_hots(q, k, first, end):
                for u in range(first, end):
                    dve.tensor_scalar(hot_s[:, k * U + u, :], iota_s[:], slot_f[:, k, u:u + 1], None, ALU.is_equal)
                    m = dve.tensor_scalar(hot_c[:, k * U + u, :], iota_c[:], col_f[:, k, u:u + 1],
                                          tok1[:, bass.ds(q * U + u, 1)], ALU.is_equal, ALU.mult)
                return m

            def route_add(q):
                dve.wait_ge(ids_ps, q + 1)
                dve.wait_ge(ids_s, q + 1)
                dve.tensor_tensor(ids[:], ids[:], ps[:, MB, 384:512], ALU.add).then_inc(ids_s, 1)

            did(dve.memset(v_ext[:], 0.0))
            dve.memset(picks[:], 0.0).then_inc(rank_ps, 1)
            dve.memset(ids[:], 0.0).then_inc(ids_s, 1)
            dve.memset(cw[:], 0.0).then_inc(cw_out, 16)
            settle()
            did(dve.memset(v_ext[:, :, HD:HD + 1], 1.0))
            dve.wait_ge(x_in[0], 16)
            ln1_stats(0)
            dve.wait_ge(bias_ps, 1)
            did(dve.tensor_copy(bias_cols[:], ps[:, PT, 0:NBR]))
            dve.wait_ge(bcast_in, 48)
            dve.wait_ge(consts, 1)
            settle()
            normalise(0, 0)
            copy_qk(0)
            copy_v(0)
            normalise(1, 0)
            for c in range(DC):
                row_max(0, c)
            copy_qk(1)
            first_steps = step[0]
            counts = []

            def counted(q, last):
                body(q, last)
                counts.append(step[0])
            groups(dve, counted)
            assert counts[1] == PER_GROUP and counts[0] == PER_GROUP - ROUTE_STEPS, counts
            for u in range(U):
                for place in range(4):
                    route(NU - 1, u, place)
            route_add(NU - 1)

            dve.wait_ge(ids_s, NU + 1)
            dve.tensor_copy(cnt_f[:], picks[:]).then_inc(run_s, 1)
            dve.wait_ge(cnt_ps, 1)
            dve.wait_ge(run_s, 1)
            did(dve.tensor_scalar(cnt_f[:], ps[:, PT + 1, 0:NE], float(ITEM - 1), None, ALU.add))
            settle()
            did(dve.tensor_copy(cnt_i[:], cnt_f[:]))
            settle()
            did(dve.tensor_scalar(cnt_i[:], cnt_i[:], ITEM.bit_length() - 1, None, ALU.arith_shift_right))
            settle()
            did(dve.tensor_scalar(items[:], cnt_i[:], 2.0, None, ALU.max))
            did(dve.tensor_scalar(more_items[:], cnt_i[:], 2.0, -1.0, ALU.max, ALU.add))
            did(dve.tensor_scalar(ids_get[:], ids[:], -1.0, 0.0, ALU.add, ALU.max))
            did(dve.tensor_scalar(ids_f[:], ids[:], 0.0, float(SKIP), ALU.is_equal, ALU.mult))
            settle()
            did(dve.scalar_tensor_tensor(ids_put[:], ids[:], -1.0, ids_f[:], ALU.add, ALU.add))
            settle()
            dve.memset(cw_now[:], 0.0).then_inc(lists, 1)

            g = dve.alloc_register("dve_item")
            dve.reg_mov(g, 1)
            pairs = dve.alloc_register("dve_pairs")
            dve.reg_mov(pairs, 0)

            def take_item(k):
                dve.wait_ge(xt_ps, k)
                for half in range(2):
                    dve.tensor_copy(cw_next[:, half, :], rows[half][:, D:ROW])
                turned = ps[:, OB, :].rearrange("p (c n) -> p c n", c=DC)
                dve.tensor_copy(xT_hi[:], turned).then_inc(xt_hi, 1)
                dve.wait_ge(xt_hi, k)
                dve.tensor_tensor(xT_lo[:], turned, xT_hi[:].bitcast(F32), ALU.subtract).then_inc(xt_sb, 1)

            dve.wait_ge(lists, 1)
            dve.memset(cw_next[:], 0.0).then_inc(xt_sb, 1)
            dve.memset(cw_now[:], 0.0).then_inc(y_s, 2)
            dve.memset(h_chunk[:], 0.0).then_inc(h_sb, 2)
            dve.wait_ge(xt_sb, 1)
            take_item(1)
            def item(e):
                k = dve.snap(g)
                hp = dve.snap(pairs)
                dve.wait_ge(xt_sb, k + 1)
                dve.wait_ge(y_s, k + 1)
                dve.tensor_copy(cw_now[:], cw_next[:]).then_inc(cw_moved, 1)
                for j in range(FC // 2):
                    two = slice(j * 2, j * 2 + 2)
                    raw = h_chunk[:, j % 2 * 2:j % 2 * 2 + 2, :]
                    dve.wait_ge(h_act, (hp + j) * 2 + 2)
                    dve.tensor_copy(hT_hi[:, two, :], raw).then_inc(h_hi, 1)
                    dve.wait_ge(h_hi, hp + j + 1)
                    dve.tensor_tensor(hT_lo[:, two, :], raw, hT_hi[:, two, :].bitcast(F32), ALU.subtract
                                      ).then_inc(h_sb, 1)
                dve.wait_ge(cw_moved, k)
                take_item(k + 1)
                dve.wait_ge(y_ps, k)
                for half in range(2):
                    m = dve.tensor_tensor(yb[:, half, :], ps[:, PT + half, 0:D],
                                          b2_bc[:, bass.ds(e, 1), :].rearrange("p o d -> p (o d)"), ALU.add)
                m.then_inc(y_b, 1)
                dve.wait_ge(y_b, k)
                dve.wait_ge(put_s, (k + 2) * 32)
                for half in range(2):
                    m = dve.tensor_scalar(yw[half][:], yb[:, half, :],
                                          cw_now[:, half, bass.ds(e, 1)], None, ALU.mult)
                m.then_inc(y_s, 1)
                dve.reg_add(g, g, 1)
                dve.reg_add(pairs, pairs, FC // 2)

            def expert(e, par):
                n = dve.value_load(items[0:1, bass.ds(e, 1)], min_val=2, max_val=N // ITEM)
                if par is not None:
                    dve.wait_ge(hi_done, e + 1)
                    dve.tensor_tensor(w2_lo[par][:], w2_raw[par][:], w2_hi[par][:].bitcast(F32), ALU.subtract
                                      ).then_inc(lo2_done, 1)
                with dve.Fori(0, n) as _i:
                    item(e)

            expert(0, None)
            with dve.Fori(0, NE // 2 - 1) as pair:
                expert(pair * 2 + 1, 1)
                expert(pair * 2 + 2, 0)
            expert(NE - 1, 1)

        @block.gpsimd
        def _(pool):
            n = [0]

            def did(m):
                n[0] += 1
                m.then_inc(pool_step, 1)

            def settle():
                pool.wait_ge(pool_step, n[0])

            did(pool.memset(ident[:], 0.0))
            did(pool.memset(head_mask[:], SCALE))
            did(pool.memset(ones_bf[:], 1.0))
            did(pool.memset(minus_half[:], -0.5))
            did(pool.iota(iota_i[:], pattern=[[1, P]], base=0, channel_multiplier=0))
            did(pool.iota(codes_i[:], pattern=[[0, U], [-1, NE]], base=NE, channel_multiplier=0))
            did(pool.iota(tok_i[:], pattern=[[P, NB]], base=1, channel_multiplier=1))
            settle()
            did(pool.affine_select(out=ident[:], in_=ident[:], compare_op=ALU.not_equal, fill=1.0, base=0,
                                   pattern=[[-1, P]], channel_multiplier=1))
            did(pool.affine_select(out=earlier[:], in_=ones_bf[:], compare_op=ALU.is_gt, fill=0.0, base=0,
                                   pattern=[[1, P]], channel_multiplier=-1))
            did(pool.affine_select(out=head_mask[:], in_=head_mask[:], compare_op=ALU.is_ge, fill=0.0, base=0,
                                   pattern=[[-HD, HC]], channel_multiplier=1))
            did(pool.tensor_copy(iota_s[:], iota_i[:]))
            did(pool.tensor_copy(codes[:], codes_i[:]))
            did(pool.tensor_copy(tok1[:], tok_i[:]))
            settle()
            did(pool.tensor_scalar(iota_c[:], iota_s[:], -float(NE * TPE), None, ALU.add))
            did(pool.affine_select(out=head_mask[:], in_=head_mask[:], compare_op=ALU.is_ge, fill=0.0, base=HD - 1,
                                   pattern=[[HD, HC]], channel_multiplier=-1))
            settle()
            pool.memset(yw[0][:], 0.0).then_inc(consts, 1)

            def ln1_rstd(q):
                pool.wait_ge(stats_done, q + 1)
                pool.tensor_tensor(rstd[:, bass.ds(q * U, U)], vare[:, bass.ds(q * U, U)], minus_half[:, 0:U], ALU.pow
                                   ).then_inc(rstd_done, 1)

            def mask_keys(b):
                pool.wait_ge(qk_sb, b + 1)
                for c in range(DC):
                    pool.tensor_tensor(kmask[:, c, :, :], qkT[:, DC + c:DC + c + 1, :].to_broadcast([P, HC, P]),
                                       head_mask[:].unsqueeze(2).to_broadcast([P, HC, P]), ALU.mult
                                       ).then_inc(kmask_s, 1)

            def body(q, last):
                if not last:
                    ln1_rstd(q + 1)
                for u in range(U):
                    b = q * U + u
                    pool.wait_ge(var2_s, b + 1)
                    pool.tensor_tensor(rstd2[:], vare2[:], minus_half[:, 0:1], ALU.pow).then_inc(rstd2_s, 1)
                    if not (last and u >= U - 2):
                        pool.wait_ge(s_ps, (b + 2) * DC)
                        mask_keys(b + 2)

            def add_rows():
                for half in range(2):
                    pool.indirect_dma_start(out_rows, bass.IndirectOffsetOnAxis(put_idx[:, half:half + 1], 0),
                                            yw[half][:], None, bounds_check=N - 1, oob_is_err=False,
                                            compute_op=ALU.add).then_inc(put_s, 16)

            for rows_of in (put_idx, put_next, put_new):
                pool.memset(rows_of[:], SKIP).then_inc(put_q, 1)
            pool.memset(yw[1][:], 0.0).then_inc(pool_step, 1)
            ln1_rstd(0)
            mask_keys(0)
            pool.wait_ge(s_ps, DC)
            mask_keys(1)
            pool.wait_ge(put_q, 3)
            pool.wait_ge(pool_step, n[0] + 1)
            pool.wait_ge(consts, 1)
            add_rows()
            groups(pool, body)

            def w1_low_part(par, e):
                wait_alone(pool, hi_done, e + 1)
                pool.tensor_tensor(w1_lo[par][:], w1_raw[par][:], w1_hi[par][:].bitcast(F32), ALU.subtract
                                   ).then_inc(lo1_done, 1)

            w1_low_part(0, 0)
            pool.tensor_tensor(w2_lo[0][:], w2_raw[0][:], w2_hi[0][:].bitcast(F32), ALU.subtract
                               ).then_inc(lo2_done, 1)
            pool.wait_ge(lists, 1)
            pool.wait_ge(xn2_out, NB * 16)
            pool.wait_ge(cw_out, (NU + 1) * 16)
            pool.wait_ge(x1_out, NB * 16)
            g = pool.alloc_register("pool_item")
            pool.reg_mov(g, 1)

            def get_rows():
                for half in range(2):
                    pool.indirect_dma_start(rows[half][:], None, table,
                                            bass.IndirectOffsetOnAxis(get_idx[:, half:half + 1], 0)
                                            ).then_inc(gat, 16)

            def put_rows(k, col):
                wait_alone(pool, put_s, k * 32)
                wait_alone(pool, put_q, k * 3)
                pool.tensor_copy(put_idx[:], put_next[:]).then_inc(put_q, 1)
                wait_alone(pool, put_q, k * 3 + 1)
                pool.tensor_copy(put_next[:], put_new[:]).then_inc(put_q, 1)
                wait_alone(pool, put_q, k * 3 + 2)
                pool.tensor_copy(put_new[:], ids_put[:, bass.ds(col, 2)]).then_inc(put_q, 1)
                wait_alone(pool, y_s, k)
                add_rows()

            def item(e, i, par=None):
                k = pool.snap(g)
                col = e * TPE + i * 2
                wait_alone(pool, xt_sb, k)
                pool.tensor_copy(get_idx[:], ids_get[:, bass.ds(col, 2)]).then_inc(idx_s, 1)
                wait_alone(pool, idx_s, k)
                get_rows()
                put_rows(k, col)
                if par is not None:
                    w1_low_part(par, e)
                pool.reg_add(g, g, 1)

            def expert(e, par):
                m = pool.value_load(more_items[0:1, bass.ds(e, 1)], min_val=1, max_val=N // ITEM - 1)
                item(e, 0, par)
                with pool.Fori(0, m) as i:
                    item(e, i + 1)

            expert(0, None)
            with pool.Fori(0, NE // 2 - 1) as pair:
                expert(pair * 2 + 1, 1)
                expert(pair * 2 + 2, 0)
            expert(NE - 1, 1)
            k = pool.snap(g)
            wait_alone(pool, xt_sb, k)
            get_rows()
            put_rows(k, 0)
            put_rows(k + 1, 0)
            wait_alone(pool, gat, k * 32)


_INS = ["x", "ctx_1024", "L0_xattn_wq", "L0_xattn_bq", "L0_xattn_wk", "L0_xattn_bk", "L0_xattn_wv", "L0_xattn_bv",
        "L0_ffn_Wg", "L0_ffn_bg", "L0_ffn_W1", "L0_ffn_b1", "L0_ffn_W2", "L0_ffn_b2"]


def kernel(**inputs):
    import numpy as _np
    import concourse.bacc as _bacc
    from concourse import mybir as _mybir
    from concourse.bass_utils import run_bass_kernel_spmd as _run

    nc = _bacc.Bacc("TRN2", target_bir_lowering=False, num_devices=1)
    arrays, args = {}, []
    for name in _INS:
        a = _np.ascontiguousarray(inputs[name])
        arrays[f"in_{name}"] = a
        args.append(nc.dram_tensor(f"in_{name}", a.shape, _mybir.dt.from_np(a.dtype), kind="ExternalInput").ap())
    shape = arrays["in_x"].shape
    args.append(nc.dram_tensor("out_0", shape, _mybir.dt.float32, kind="ExternalOutput").ap())
    build_xattn_moe(nc, *args)
    r = _run(nc, [arrays], core_ids=[0])
    return r.results[0]["out_0"]
```

```python
from contextlib import ExitStack

import concourse.bass as bass
from concourse import mybir

P = 128
ALU = mybir.AluOpType
ACT = mybir.ActivationFunctionType
AX_X = mybir.AxisListType.X
F32 = mybir.dt.float32
F32R = mybir.dt.float32r
F16 = mybir.dt.float16
BF16 = mybir.dt.bfloat16
I32 = mybir.dt.int32


def build_xattn_moe(nc, x, ctx_in, wq, bq, wk, bk, wv, bv, wg, bg, w1, b1, w2, b2, out):
    NB, S, D = x.shape
    NE, _, F = w1.shape
    HEADS = 16
    HD = D // HEADS
    DC = D // P
    FC = F // P
    HC = HEADS // DC
    GH = 4
    NG = HEADS // GH
    VW = 32
    U = 4
    NU = NB // U
    N = NB * S
    TPE = N // P
    ITEM = 2 * P
    ROW = D + NE
    SKIP = 2 * N
    SCALE = 1.0 / HD ** 0.5
    TOPK = 2
    ln1_ends = [0, 1] + list(range(U, NB + 1, U))
    assert S == P and NU >= 2 and NE == 8
    assert HD in (4, 16, 64)

    x_v = x.rearrange("b s d -> s b d")
    out_rows = out.rearrange("b s d -> (b s) d")
    w1_v = w1.rearrange("e (c p) f -> e p c f", p=P)
    w2_v = w2.rearrange("e (c p) d -> e p c d", p=P)
    table = nc.dram_tensor("token_table", [N, ROW], F32).ap()
    table_v = table.rearrange("(b s) d -> b s d", s=S)

    with ExitStack() as stack:
        def sb(name, shape, dt=F32):
            return stack.enter_context(nc.sbuf_tensor(name, shape, dt))

        def sem(name):
            return stack.enter_context(nc.semaphore(name))

        ident = sb("ident", [P, P])
        head_mask = sb("head_mask", [P, HC])
        earlier = sb("earlier", [P, P], BF16)
        ones_bf = sb("ones_bf", [P, P], BF16)
        iota_s = sb("iota_s", [P, P], F16)
        iota_c = sb("iota_c", [P, P], F16)
        codes = sb("codes", [P, U, NE])
        iota_i = sb("iota_i", [P, P], I32)
        codes_i = sb("codes_i", [P, U, NE], I32)
        tok_i = sb("tok_i", [P, NB], I32)
        tok1 = sb("tok1", [P, NB])
        minus_half = sb("minus_half", [P, NB])
        wq_sb = sb("wq_sb", [P, DC, D])
        wk_sb = sb("wk_sb", [P, DC, D])
        wv_sb = sb("wv_sb", [P, DC, D])
        wg_sb = sb("wg_sb", [P, DC, NE])
        bv_bc = sb("bv_bc", [P, D])
        bg_bc = sb("bg_bc", [P, NE])
        b2_bc = sb("b2_bc", [P, NE, D])
        NBR = NE * FC + 2 * DC
        bias_rows = sb("bias_rows", [NBR, P])
        bias_cols = sb("bias_cols", [P, NBR])

        x_all = sb("x_all", [P, NB, D])
        ctx_sb = [sb(f"ctx_sb{i}", [P, D]) for i in range(2)]
        stats = sb("stats", [P, NB, 6])
        mv = sb("mv", [P, NB, 2])
        mean = sb("mean", [P, NB])
        rstd = sb("rstd", [P, NB])
        vare = sb("vare", [P, NB])
        xn = sb("xn", [P, D])
        xcT = sb("xcT", [P, 2 * DC, P])
        qkT = sb("qkT", [P, 2 * DC, P])
        qk_hi = sb("qk_hi", [P, 2 * DC, P], F32R)
        qk_lo = sb("qk_lo", [P, 2 * DC, P], F32R)
        kmask_hi = sb("kmask_hi", [P, DC, HC, P], F32R)
        kmask_lo = sb("kmask_lo", [P, DC, HC, P], F32R)
        v_ext = sb("v_ext", [P, HEADS, VW])
        negmax = sb("negmax", [P, HEADS])
        probs = sb("probs", [P, HEADS, P])
        pT = sb("pT", [P, 2, GH, P])
        oT_sb = sb("oT_sb", [P, NG, P])
        inv_sum = sb("inv_sum", [P, HEADS])
        att = sb("att", [P, D])
        x1 = sb("x1", [P, D])
        stats2 = sb("stats2", [P, 6])
        mv2 = sb("mv2", [P, 2])
        vare2 = sb("vare2", [P, 1])
        rstd2 = sb("rstd2", [P, 1])
        xn2 = sb("xn2", [P, D])
        xn2T = sb("xn2T", [P, DC, P])
        lg = sb("lg", [P, U, NE])
        lgs = sb("lgs", [P, U, NE])
        ex = sb("ex", [P, U, NE])
        lgm = sb("lgm", [P, U, NE])
        eq = sb("eq", [P, U, NE])
        biggest = sb("biggest", [P, TOPK, U])
        ex_sum = sb("ex_sum", [P, U])
        den = sb("den", [P, U])
        inv_den = sb("inv_den", [P, U])
        top = sb("top", [P, TOPK, U])
        code = sb("code", [P, TOPK, U])
        onehot = sb("onehot", [P, TOPK, U, NE])
        ohr = sb("ohr", [P, TOPK, U, NE])
        oht = sb("oht", [P, TOPK, U, NE])
        ohw = sb("ohw", [P, TOPK, U, NE])
        wtop = sb("wtop", [P, TOPK, U])
        cw = sb("cw", [P, U, NE])
        picked = sb("picked", [P, U, NE], BF16)
        run = sb("run", [P, NE], BF16)
        picks = sb("picks", [P, NE], BF16)
        pick_sums = sb("pick_sums", [P, 2, NE], BF16)
        rank = sb("rank", [P, TOPK, U])
        rank_i = sb("rank_i", [P, TOPK, U], I32)
        tile_i = sb("tile_i", [P, TOPK, U], I32)
        slot_i = sb("slot_i", [P, TOPK, U], I32)
        slot_f = sb("slot_f", [P, TOPK, U])
        col_f = sb("col_f", [P, TOPK, U])
        hot_s = sb("hot_s", [P, TOPK * U, P], F16)
        hot_c = sb("hot_c", [P, TOPK * U, P], F16)
        ids = sb("ids", [P, NE * TPE])
        ids_f = sb("ids_f", [P, NE * TPE])
        ids_get = sb("ids_get", [P, NE * TPE], I32)
        ids_put = sb("ids_put", [P, NE * TPE], I32)
        cnt_f = sb("cnt_f", [P, NE])
        tiles_f = sb("tiles_f", [P, NE])
        cnt_i = sb("cnt_i", [P, NE], I32)
        items = sb("items", [P, NE], I32)
        more_items = sb("more_items", [P, NE], I32)
        tiles_of = sb("tiles_of", [P, NE], I32)
        last_full = sb("last_full", [P, NE], I32)
        pe_plan = sb("pe_plan", [P, NE], I32)
        w1_raw = [sb(f"w1_raw{i}", [P, DC, F]) for i in range(2)]
        w2_raw = [sb(f"w2_raw{i}", [P, FC, D]) for i in range(2)]
        w1_hi = [sb(f"w1_hi{i}", [P, DC, F], F32R) for i in range(2)]
        w2_hi = [sb(f"w2_hi{i}", [P, FC, D], F32R) for i in range(2)]
        w1_lo = [sb(f"w1_lo{i}", [P, DC, F], F32R) for i in range(2)]
        w2_lo = [sb(f"w2_lo{i}", [P, FC, D], F32R) for i in range(2)]
        get_idx = sb("get_idx", [P, 2], I32)
        put_new = sb("put_new", [P, 2], I32)
        put_next = sb("put_next", [P, 2], I32)
        put_idx = sb("put_idx", [P, 2], I32)
        rows0 = sb("rows0", [P, ROW])
        rows1 = sb("rows1", [P, ROW])
        rows = [rows0, rows1]
        cw_next = sb("cw_next", [P, 2, NE])
        cw_now = sb("cw_now", [P, 2, NE])
        xT_hi = sb("xT_hi", [P, DC, ITEM], F32R)
        xT_lo = sb("xT_lo", [P, DC, ITEM], F32R)
        act_table = sb("act_table", [P, 1])
        act_out = sb("act_out", [P, 1])
        bias_now = [sb(f"bias_now{i}", [P, FC]) for i in range(2)]
        h_chunk = sb("h_chunk", [P, 4, ITEM])
        assert FC * ITEM == DC * HC * P
        hT_hi, hT_lo = (k[:].rearrange("p c h n -> p (c h n)").rearrange("p (f n) -> p f n", f=FC)
                        for k in (kmask_hi, kmask_lo))
        yb = sb("yb", [P, 2, D])
        yw0 = sb("yw0", [P, D])
        yw1 = sb("yw1", [P, D])
        yw = [yw0, yw1]

        ps = stack.enter_context(nc.psum_tensor("ps", [P, 8, 512], F32))
        PT, OB, MB = 4, 6, 7
        LG = D
        RK = LG + U * NE
        IDS = 512 - NE * TPE

        x_in = [sem("x_of_batch_0_loaded"), sem("x_of_group_0_loaded"), sem("other_x_loaded")]
        ctx_s = [sem("even_ctx_loaded"), sem("odd_ctx_loaded")]
        wqk_in = sem("query_key_weights_loaded")
        wv_in = sem("value_router_weights_loaded")
        small_in = sem("bias_rows_loaded")
        bcast_in = sem("broadcast_biases_loaded")
        b2_in = sem("b2_loaded")
        consts = sem("constants_built")
        pool_step = sem("pool_step")
        bias_ps = sem("biases_transposed")
        dve_step = sem("dve_step")
        stats_done = sem("ln1_stats_done")
        rstd_done = sem("ln1_rstd_done")
        xn_done = sem("xn_done")
        xcT_ps = sem("xcT_in_psum")
        xcT_sb = sem("xcT_in_sbuf")
        qk_ps = sem("qk_in_psum")
        qk_sb = sem("qk_in_sbuf")
        qk_hi_s = sem("qk_high_parts_done")
        qk_lo_s = sem("qk_low_parts_done")
        v_ps = sem("v_in_psum")
        v_sb = sem("v_in_sbuf")
        kmask_s = sem("kmask_done")
        kmask_first_s = sem("kmask_of_batch_0_done_by_dve")
        table_s = sem("act_table_input_written")
        s_ps = sem("scores_in_psum")
        max_s = sem("negmax_done")
        exp_s = sem("probs_done")
        pT_ps = sem("pT_in_psum")
        pT_dve = sem("pT_copied_by_dve")
        pT_act = sem("pT_copied_by_act")
        pv_s = sem("pv_in_psum")
        o_sb = sem("oT_in_sbuf")
        o_ps = sem("o_in_psum")
        x1_s = sem("x1_done")
        x1_out = sem("x1_stored")
        var2_s = sem("ln2_var_done")
        rstd2_s = sem("ln2_rstd_done")
        xn2_s = sem("xn2_done")
        xn2_out = sem("xn2_stored")
        xn2T_ps = sem("xn2T_in_psum")
        xn2T_sb = sem("xn2T_in_sbuf")
        lg_ps = sem("logits_in_psum")
        lg_read = sem("logits_read")
        lg_s = sem("logits_shifted")
        ex_s = sem("router_exp_done")
        cw_s = sem("combine_weights_done")
        cw_out = sem("combine_weights_stored")
        pick_s = sem("choices_done")
        rank_read = sem("ranks_read")
        rank_ps = sem("ranks_in_psum")
        hot_done = sem("onehots_done")
        ids_ps = sem("ids_in_psum")
        ids_s = sem("ids_added")
        run_s = sem("totals_done")
        cnt_ps = sem("counts_in_psum")
        gets_listed = sem("rows_to_gather_listed")
        lists = sem("lists_ready")
        w_in = [sem("ffn_weights0_loaded"), sem("ffn_weights1_loaded")]
        idx_s = sem("gather_indices_copied")
        gat = sem("rows_gathered")
        xt_ps = sem("item_transposed")
        xt_sb = sem("item_in_sbuf")
        h_ps = sem("hidden_in_psum")
        h_act = sem("hidden_gelu_done")
        hi_done = sem("weights_high_parts_done")
        lo1_done = sem("w1_low_part_done")
        lo2_done = sem("w2_low_part_done")
        bias_s = sem("expert_bias_copied")
        xt_hi = sem("item_high_part_done")
        h_hi = sem("hidden_high_parts_done")
        h_sb = sem("hidden_pairs_split")
        y_ps = sem("y_in_psum")
        y_b = sem("y_biased")
        y_s = sem("y_scaled")
        cw_moved = sem("cw_moved")
        put_s = sem("rows_added")
        put_q = sem("put_queue_moved")

        block = stack.enter_context(nc.Block())

        wait_registers = {}

        def wait_alone(eng, signal, value):
            if not isinstance(value, int):
                if eng.engine not in wait_registers:
                    wait_registers[eng.engine] = eng.alloc_register(f"wait_value_{len(wait_registers)}")
                eng.reg_mov(wait_registers[eng.engine], value)
                value = wait_registers[eng.engine]
            eng.wait_ge(consts, 1)
            eng.wait_ge(signal, value)

        def groups(eng, body):
            body(0, False)
            with eng.Fori(1, NU - 1) as q:
                body(q, False)
            body(NU - 1, True)

        @block.sync
        def _(sp):
            sp.dma_start(x_all[:, 0:1, :], x_v[:, 0:1, :]).then_inc(x_in[0], 16)
            sp.dma_start(ctx_sb[0][:], ctx_in[0]).then_inc(ctx_s[0], 16)
            sp.dma_start(wq_sb[:], wq.rearrange("(c p) n -> p c n", p=P)).then_inc(wqk_in, 16)
            sp.dma_start(wk_sb[:], wk.rearrange("(c p) n -> p c n", p=P)).then_inc(wqk_in, 16)
            sp.dma_start(x_all[:, 1:U, :], x_v[:, 1:U, :]).then_inc(x_in[1], 16)
            sp.dma_start(ctx_sb[1][:], ctx_in[1]).then_inc(ctx_s[1], 16)
            sp.dma_start(bv_bc[:], bv.partition_broadcast(P)).then_inc(bcast_in, 16)
            sp.dma_start(bg_bc[:], bg.partition_broadcast(P)).then_inc(bcast_in, 16)
            sp.dma_start(x_all[:, U:, :], x_v[:, U:, :]).then_inc(x_in[2], 16)
            for par in range(2):
                sp.dma_start(w1_raw[par][:], w1_v[par]).then_inc(w_in[par], 16)
                sp.dma_start(w2_raw[par][:], w2_v[par]).then_inc(w_in[par], 16)
            sp.dma_start(b2_bc[:], b2.partition_broadcast(P)).then_inc(b2_in, 16)
            sp.wait_ge(xcT_ps, 1)
            sp.dma_start(ctx_sb[0][:], ctx_in[2]).then_inc(ctx_s[0], 16)

            def store_cw(q):
                sp.wait_ge(cw_s, q + 1)
                sp.dma_start(table_v[bass.ds(q * U, U), :, D:ROW].rearrange("b s e -> s b e"),
                             cw[:]).then_inc(cw_out, 16)

            def body(q, last):
                for u in range(U):
                    b = q * U + u
                    sp.wait_ge(x1_s, b + 1)
                    sp.dma_start(out[bass.ds(b, 1)].rearrange("o s d -> (o s) d"), x1[:]).then_inc(x1_out, 16)
                    sp.wait_ge(xn2_s, b + 1)
                    sp.dma_start(table_v[bass.ds(b, 1), :, 0:D].rearrange("o s d -> (o s) d"),
                                 xn2[:]).then_inc(xn2_out, 16)
                    if not (last and u >= U - 3):
                        sp.wait_ge(xcT_ps, b + 2)
                        sp.dma_start(ctx_sb[(u + 1) % 2][:], ctx_in[bass.ds(b + 3, 1)].rearrange("o s d -> (o s) d")
                                     ).then_inc(ctx_s[(u + 1) % 2], 16)
                    if u == 3 and not (isinstance(q, int) and q == 0):
                        store_cw(q - 1)
            groups(sp, body)
            store_cw(NU - 1)

            sp.wait_ge(x1_out, NB * 16)
            sp.wait_ge(xn2_out, NB * 16)
            sp.wait_ge(cw_out, (NU + 1) * 16)
            sp.wait_ge(gat, 32)
            with sp.Fori(0, NE // 2 - 1) as pair:
                for par in range(2):
                    sp.wait_ge(lo1_done, pair * 2 + (par + 1))
                    sp.wait_ge(lo2_done, pair * 2 + (par + 1))
                    e = pair * 2 + (par + 2)
                    sp.dma_start(w1_raw[par][:], w1_v[bass.ds(e, 1)].rearrange("o p c f -> (o p) c f")
                                 ).then_inc(w_in[par], 16)
                    sp.dma_start(w2_raw[par][:], w2_v[bass.ds(e, 1)].rearrange("o p c d -> (o p) c d")
                                 ).then_inc(w_in[par], 16)
            sp.wait_ge(lists, 1)
            done = sp.alloc_register("sp_items_done")
            sp.reg_mov(done, 0)
            for e in range(NE):
                n = sp.value_load(items[0:1, e:e + 1], min_val=2, max_val=N // ITEM)
                sp.reg_add(done, done, n)
            total = sp.snap(done)
            wait_alone(sp, put_s, (total + 3) * 32)

        @block.tensor
        def _(pe):
            def rank_group(q):
                pe.wait_ge(pick_s, q + 1)
                rk = ps[:, PT + 1, RK:RK + U * NE]
                pk = picked[:].rearrange("p u e -> p (u e)")
                pe.matmul(rk, earlier[:], pk, start=True, stop=False)
                for d in range(1, U):
                    pe.matmul(rk[:, d * NE:], ones_bf[:], pk[:, :(U - d) * NE], start=False, stop=False)
                for u in range(U):
                    m = pe.matmul(rk[:, u * NE:(u + 1) * NE], ones_bf[:], run[:], start=False, stop=(u == U - 1))
                m.then_inc(rank_ps, 1)

            def place_ids(q):
                pe.wait_ge(hot_done, q + 1)
                for k in range(TOPK * U):
                    m = pe.matmul(ps[:, PT + 1, IDS:512], hot_s[:, k, :], hot_c[:, k, :],
                                  start=(k == 0), stop=(k == TOPK * U - 1))
                m.then_inc(ids_ps, 1)

            def turn_inputs(b, par, loads):
                pe.wait_ge(consts, 1)
                pe.wait_ge(xn_done, b + 1)
                pe.wait_ge(ctx_s[par], loads * 16)
                if not (isinstance(b, int) and b == 0):
                    pe.wait_ge(v_sb, b)
                for j in range(2 * DC):
                    src = xn if j < DC else ctx_sb[par]
                    m = pe.transpose(ps[:, MB, j * P:(j + 1) * P], src[:, (j % DC) * P:(j % DC + 1) * P], ident[:])
                m.then_inc(xcT_ps, 1)

            def project_qk(b):
                pe.wait_ge(xcT_sb, b + 1)
                if isinstance(b, int) and b == 0:
                    pe.wait_ge(wqk_in, 32)
                for j in range(2 * DC):
                    w = wq_sb if j < DC else wk_sb
                    src = 0 if j < DC else DC
                    for c in range(DC):
                        m = pe.matmul(ps[:, OB, j * P:(j + 1) * P], w[:, c, (j % DC) * P:(j % DC + 1) * P],
                                      xcT[:, src + c, :], start=(c == 0), stop=(c == DC - 1))
                m.then_inc(qk_ps, 1)

            def project_v(b):
                if isinstance(b, int) and b == 0:
                    pe.wait_ge(wv_in, 32)
                for c in range(DC):
                    m = pe.matmul(ps[:, MB, 0:D], xcT[:, DC + c, :], wv_sb[:, c, :],
                                  start=(c == 0), stop=(c == DC - 1))
                m.then_inc(v_ps, 1)

            def scores(b, banks=range(NG)):
                for g in banks:
                    c, first = g * DC // NG, g % (NG // DC) * GH
                    if not (isinstance(b, int) and b == 0):
                        pe.wait_ge(kmask_s, b * DC + c + 1)
                    elif c == 0:
                        pe.wait_ge(kmask_s, DC)
                    else:
                        pe.wait_ge(kmask_first_s, c)
                    k_hi, k_lo = (k[:, c, first:first + GH, :] for k in (kmask_hi, kmask_lo))
                    pe.matmul(ps[:, g, :], qk_lo[:, c, :], k_hi, start=True, stop=False)
                    pe.matmul(ps[:, g, :], qk_hi[:, c, :], k_lo, start=False, stop=False)
                    pe.matmul(ps[:, g, :], qk_hi[:, c, :], k_hi, start=False, stop=True).then_inc(s_ps, 1)

            def logits(b, u):
                for c in range(DC):
                    m = pe.matmul(ps[:, PT + 1, LG + u * NE:LG + (u + 1) * NE], xn2T[:, c, :], wg_sb[:, c, :],
                                  start=(c == 0), stop=(c == DC - 1))
                m.then_inc(lg_ps, 1)

            def pT_copied(b, g):
                if g == 0:
                    pe.wait_ge(pT_dve, b + 1)
                else:
                    pe.wait_ge(pT_act, b * (NG - 1) + g)

            def turn_probs(b, g):
                pe.wait_ge(exp_s, b * NG + g + 1)
                if g >= 2:
                    pT_copied(b, g - 2)
                elif g == 1 and not (isinstance(b, int) and b == 0):
                    pe.wait_ge(lg_read, b)
                for i in range(GH):
                    m = pe.transpose(ps[:, PT + g % 2, i * P:(i + 1) * P], probs[:, g * GH + i, :], ident[:])
                m.then_inc(pT_ps, 1)

            def times_v(b, g, more1):
                pT_copied(b, g)
                if g == 0:
                    pe.wait_ge(v_sb, b + 1)
                    if more1:
                        pe.wait_ge(qk_sb, b + 2)
                for i in range(GH):
                    m = pe.matmul(ps[i * VW:(i + 1) * VW, OB, g * P:(g + 1) * P],
                                  v_ext[:, g * GH + i, :], pT[:, g % 2, i, :], start=True, stop=True,
                                  tile_position=(0, i * VW))
                m.then_inc(pv_s, 1)

            def body(q, last):
                for u in range(U):
                    b = q * U + u
                    more1 = not (last and u >= U - 1)
                    more2 = not (last and u >= U - 2)
                    turn_probs(b, 0)
                    if not (isinstance(q, int) and q == 0 and u == 0):
                        pe.wait_ge(xn2T_sb, b)
                        if u in (0, 2) and not (isinstance(q, int) and q == 0):
                            (place_ids if u == 0 else rank_group)(q - 1)
                        logits(b - 1, (u - 1) % U)
                    if more1:
                        project_v(b + 1)
                    if u in (0, 2) and not (isinstance(q, int) and q == 0):
                        pe.wait_ge(ids_s if u == 0 else rank_read, q)
                    turn_probs(b, 1)
                    for g in range(NG):
                        times_v(b, g, more1)
                        if g + 2 < NG:
                            turn_probs(b, g + 2)
                    if more1:
                        scores(b + 1, [0])
                    if more2:
                        turn_inputs(b + 2, u % 2, q * (U // 2) + (u // 2 + 2))
                    pe.wait_ge(o_sb, b + 1)
                    for g in range(NG):
                        m = pe.transpose(ps[:, PT, g * P:(g + 1) * P], oT_sb[:, g, :], ident[:])
                    m.then_inc(o_ps, 1)
                    if more1:
                        scores(b + 1, [1])
                    if more2:
                        project_qk(b + 2)
                    if more1:
                        scores(b + 1, range(2, NG))
                    if last and u == U - 1:
                        place_ids(q)
                        pe.wait_ge(ids_s, NU)
                    pe.wait_ge(xn2_s, b + 1)
                    for c in range(DC):
                        m = pe.transpose(ps[:, PT + 1, c * P:(c + 1) * P], xn2[:, c * P:(c + 1) * P], ident[:])
                    m.then_inc(xn2T_ps, 1)

            pe.wait_ge(consts, 1)
            pe.wait_ge(small_in, 48)
            pe.transpose(ps[:, PT, 0:NBR], bias_rows[:], ident[0:NBR, 0:NBR]).then_inc(bias_ps, 1)
            turn_inputs(0, 0, 1)
            project_qk(0)
            project_v(0)
            turn_inputs(1, 1, 1)
            scores(0)
            project_qk(1)
            groups(pe, body)
            pe.wait_ge(xn2T_sb, NB)
            logits(NB - 1, U - 1)
            rank_group(NU - 1)
            pe.wait_ge(run_s, 1)
            pe.matmul(ps[:, PT, 0:NE], ones_bf[:], picks[:], start=True, stop=True).then_inc(cnt_ps, 1)
            place_ids(NU)

            g = pe.alloc_register("pe_item")
            pe.reg_mov(g, 1)
            chunks = pe.alloc_register("pe_chunks")
            pe.reg_mov(chunks, 0)
            pairs = pe.alloc_register("pe_pairs")
            pe.reg_mov(pairs, 0)

            def turn_item(k):
                pe.wait_ge(gat, k * 32)
                pe.wait_ge(xt_sb, k)
                for half in range(2):
                    for c in range(DC):
                        m = pe.transpose(ps[:, OB, c * ITEM + half * P:c * ITEM + (half + 1) * P],
                                         rows[half][:, c * P:(c + 1) * P], ident[:])
                m.then_inc(xt_ps, 1)

            second_half = pe.alloc_register("pe_second_half")

            def first_product(par, k, hc):
                pe.wait_ge(xt_hi, k)
                for f in range(FC):
                    if f >= 4:
                        pe.wait_ge(h_act, hc + f - 3)
                    hidden = ps[:, f % 4, 0:ITEM]
                    w_hi, w_lo = (w[par][:, :, f * P:(f + 1) * P] for w in (w1_hi, w1_lo))
                    for c in range(DC):
                        pe.matmul(hidden, w_hi[:, c, :], xT_hi[:, c, :], start=(c == 0), stop=False)
                        pe.matmul(hidden, w_lo[:, c, :], xT_hi[:, c, :], start=False, stop=False)
                    if f == 0:
                        pe.wait_ge(xt_sb, k + 1)
                    for c in range(DC):
                        m = pe.matmul(hidden, w_hi[:, c, :], xT_lo[:, c, :], start=False, stop=(c == DC - 1))
                    m.then_inc(h_ps, 1)

            def second_product(par, halves, hp):
                for f in range(FC):
                    if f % 2 == 0:
                        pe.wait_ge(h_sb, hp + f // 2 + 3)
                    for half in halves:
                        y = ps[:, PT + half, 0:D]
                        h_hi_f, h_lo_f = (h[:, f, half * P:(half + 1) * P] for h in (hT_hi, hT_lo))
                        pe.matmul(y, h_lo_f, w2_hi[par][:, f, :], start=(f == 0), stop=False)
                        pe.matmul(y, h_hi_f, w2_lo[par][:, f, :], start=False, stop=False)
                        m = pe.matmul(y, h_hi_f, w2_hi[par][:, f, :], start=False, stop=(f == FC - 1))
                return m

            def item(pair, par, last):
                k = pe.snap(g)
                hp = pe.snap(pairs)
                first_product(par, k, pe.snap(chunks))
                turn_item(k + 1)
                pe.wait_ge(lo2_done, pair * 2 + (par + 1))
                pe.wait_ge(y_s, k + 1)
                if last:
                    with pe.If_ne(second_half, 0):
                        second_product(par, [1], hp)
                    second_product(par, [0], hp).then_inc(y_ps, 1)
                else:
                    second_product(par, [0, 1], hp).then_inc(y_ps, 1)
                pe.reg_add(g, g, 1)
                pe.reg_add(chunks, chunks, FC)
                pe.reg_add(pairs, pairs, FC // 2)

            pe.wait_ge(lists, 1)
            turn_item(1)
            with pe.Fori(0, NE // 2) as pair:
                for par in range(2):
                    expert = bass.ds(pair * 2 + par, 1)
                    plan = pe.value_load(pe_plan[0:1, expert], min_val=2, max_val=N // ITEM * 2 - 1)
                    n = plan // 2
                    pe.reg_mov(second_half, plan % 2)
                    wait_alone(pe, lo1_done, pair * 2 + (par + 1))
                    with pe.Fori(0, n) as _i:
                        item(pair, par, False)
                    item(pair, par, True)

        @block.scalar
        def _(act):
            act.dma_start(bias_rows[0:NE * FC, :], b1.rearrange("e (f p) -> (e f) p", p=P)).then_inc(small_in, 16)
            act.dma_start(bias_rows[NE * FC:NE * FC + DC, :], bq.rearrange("(c p) -> c p", p=P)).then_inc(small_in, 16)
            act.dma_start(bias_rows[NE * FC + DC:NBR, :], bk.rearrange("(c p) -> c p", p=P)).then_inc(small_in, 16)
            act.wait_ge(table_s, 1)
            act.activation(act_out[:], act_table[:], ACT.Exp)
            act.dma_start(wv_sb[:], wv.rearrange("(c p) n -> p c n", p=P)).then_inc(wv_in, 16)
            act.dma_start(wg_sb[:], wg.rearrange("(c p) n -> p c n", p=P)).then_inc(wv_in, 16)

            def copy_xcT(b):
                act.wait_ge(xcT_ps, b + 1)
                act.copy(xcT[:], ps[:, MB, :].rearrange("p (j n) -> p j n", j=2 * DC)).then_inc(xcT_sb, 1)

            def round_weights(par, loads):
                act.wait_ge(w_in[par], loads)
                act.copy(w1_hi[par][:], w1_raw[par][:])
                act.copy(w2_hi[par][:], w2_raw[par][:]).then_inc(hi_done, 1)

            def router_exp(q):
                act.wait_ge(lg_s, q + 1)
                act.activation(ex[:], lgs[:], ACT.Exp).then_inc(ex_s, 1)

            def round_qk(b):
                act.wait_ge(qk_sb, b + 1)
                if not (isinstance(b, int) and b == 0):
                    act.wait_ge(kmask_s, b * DC)
                    act.wait_ge(s_ps, b * NG)
                act.copy(qk_hi[:], qkT[:]).then_inc(qk_hi_s, 1)

            def exp_probs(b, groups_of_heads=range(NG)):
                for g in groups_of_heads:
                    act.wait_ge(max_s, b * NG + g + 1)
                    for h in range(g * GH, (g + 1) * GH):
                        m = act.activation(probs[:, h, :], ps[:, g, (h % GH) * P:(h % GH + 1) * P], ACT.Exp,
                                           bias=negmax[:, h:h + 1])
                    m.then_inc(exp_s, 1)

            def body(q, last):
                for u in range(U):
                    b = q * U + u
                    for g in range(1, NG):
                        act.wait_ge(pT_ps, b * NG + g + 1)
                        if g >= 2:
                            act.wait_ge(pv_s, b * NG + g - 1)
                        act.copy(pT[:, g % 2, :, :], ps[:, PT + g % 2, :].rearrange("p (i n) -> p i n", i=GH)
                                 ).then_inc(pT_act, 1)
                    act.wait_ge(pv_s, (b + 1) * NG)
                    act.copy(oT_sb[:], ps[:, OB, :].rearrange("p (g n) -> p g n", g=NG)).then_inc(o_sb, 1)
                    if not (last and u >= U - 2):
                        copy_xcT(b + 2)
                    if not (last and u >= U - 1):
                        exp_probs(b + 1, range(NG // 2))
                    act.wait_ge(xn2T_ps, b + 1)
                    act.copy(xn2T[:], ps[:, PT + 1, 0:D].rearrange("p (c n) -> p c n", c=DC)).then_inc(xn2T_sb, 1)
                    if not (last and u >= U - 2):
                        round_qk(b + 2)
                    if not (last and u >= U - 1):
                        exp_probs(b + 1, range(NG // 2, NG))
                    if u == 0 and not (isinstance(q, int) and q == 0):
                        router_exp(q - 1)
                    if last and u == U - 2:
                        round_weights(0, 32)

            copy_xcT(0)
            round_qk(0)
            copy_xcT(1)
            exp_probs(0)
            round_qk(1)
            groups(act, body)
            router_exp(NU - 1)

            g = act.alloc_register("act_chunks")
            act.reg_mov(g, 0)

            def gelu_item(par):
                k = act.snap(g)
                for f in range(FC):
                    act.wait_ge(h_ps, k + f + 1)
                    if f % 2 == 0:
                        act.wait_ge(h_sb, act.snap(p) + f // 2 + 1)
                    act.activation(h_chunk[:, f % 4, :], ps[:, f % 4, 0:ITEM], ACT.Gelu_apprx_tanh,
                                   bias=bias_now[par][:, f:f + 1]).then_inc(h_act, 1)
                act.reg_add(g, g, FC)
                act.reg_add(p, p, FC // 2)

            def expert(e, pair, par, last):
                n = act.value_load(more_items[0:1, bass.ds(e, 1)], min_val=1, max_val=N // ITEM - 1)
                act.wait_ge(bias_s, e + 1)
                gelu_item(par)
                if not last:
                    round_weights(1 - par, (pair + par + 1) * 32)
                with act.Fori(0, n) as _i:
                    gelu_item(par)

            p = act.alloc_register("act_pairs")
            act.reg_mov(p, 0)
            act.activation(act_out[:], act_table[:], ACT.Gelu_apprx_tanh)
            act.wait_ge(lists, 1)
            with act.Fori(0, NE // 2 - 1) as pair:
                for par in range(2):
                    expert(pair * 2 + par, pair, par, False)
            for par in range(2):
                expert(NE - 2 + par, NE // 2 - 1, par, par == 1)

        @block.vector
        def _(dve):
            ROUTE_STEPS = 31
            PER_GROUP = 4 * U + ROUTE_STEPS
            FIRST_GROUP = 4 * U + (NU - 2) * (2 * U + 1)
            step = [0]
            base = [0]

            def did(m):
                step[0] += 1
                m.then_inc(dve_step, 1)

            def settle(own=False):
                if own:
                    wait_alone(dve, dve_step, base[0] + step[0])
                else:
                    dve.wait_ge(dve_step, base[0] + step[0])

            def ln1_stats(part):
                first, end = ln1_ends[part], ln1_ends[part + 1]
                for b in range(first, end):
                    did(dve.bn_stats(stats[:, b, :], x_all[:, b, :]))
                settle()
                for b in range(first, end):
                    did(dve.bn_aggr(mv[:, b, :], stats[:, b, :]))
                settle()
                did(dve.tensor_copy(mean[:, first:end], mv[:, first:end, 0:1].rearrange("p b o -> p (b o)")))
                dve.tensor_scalar(vare[:, first:end], mv[:, first:end, 1:2].rearrange("p b o -> p (b o)"),
                                  1e-5, None, ALU.add).then_inc(stats_done, 1)

            def normalise(b):
                first_part = isinstance(b, int) and b < 2 * U
                dve.wait_ge(rstd_done, [i for i, end in enumerate(ln1_ends) if end > b][0] if first_part else NU + 1)
                if not (isinstance(b, int) and b == 0):
                    dve.wait_ge(xcT_ps, b)
                dve.tensor_scalar(xn[:], x_all[:, bass.ds(b, 1), :].rearrange("p o d -> p (o d)"),
                                  mean[:, bass.ds(b, 1)], rstd[:, bass.ds(b, 1)],
                                  ALU.subtract, ALU.mult).then_inc(xn_done, 1)

            def copy_qk(b):
                dve.wait_ge(qk_ps, b + 1)
                if not (isinstance(b, int) and b == 0):
                    dve.wait_ge(qk_lo_s, b)
                dve.tensor_tensor(qkT[:], ps[:, OB, :].rearrange("p (j n) -> p j n", j=2 * DC),
                                  bias_cols[:, NE * FC:NBR].unsqueeze(2).to_broadcast([P, 2 * DC, P]),
                                  ALU.add).then_inc(qk_sb, 1)

            def split_qk(b):
                dve.wait_ge(qk_hi_s, b + 1)
                if not (isinstance(b, int) and b == 0):
                    dve.wait_ge(s_ps, b * NG)
                dve.tensor_tensor(qk_lo[:], qkT[:], qk_hi[:].bitcast(F32), ALU.subtract).then_inc(qk_lo_s, 1)

            def copy_v(b):
                dve.wait_ge(v_ps, b + 1)
                if not (isinstance(b, int) and b == 0):
                    dve.wait_ge(pv_s, b * NG)
                dve.tensor_tensor(v_ext[:, :, 0:HD], ps[:, MB, 0:D].rearrange("p (h n) -> p h n", h=HEADS),
                                  bv_bc[:].rearrange("p (h n) -> p h n", h=HEADS), ALU.add).then_inc(v_sb, 1)

            def row_max(b, g):
                dve.wait_ge(s_ps, b * NG + g + 1)
                if g == 0 and not (isinstance(b, int) and b == 0):
                    dve.wait_ge(exp_s, b * NG)
                dve.tensor_reduce(negmax[:, g * GH:(g + 1) * GH],
                                  ps[:, g, :].rearrange("p (h n) -> p h n", h=GH),
                                  AX_X, ALU.max, negate=True).then_inc(max_s, 1)

            def body(q, last):
                step[0] = 0
                base[0] = first_steps + (0 if isinstance(q, int) and q == 0 else
                                         q * PER_GROUP + FIRST_GROUP - PER_GROUP)
                for u in range(U):
                    b = q * U + u
                    more1 = not (last and u >= U - 1)
                    more2 = not (last and u >= U - 2)
                    if not (isinstance(q, int) and q == 0 and u == 0):
                        read_logits(b - 1, (u - 1) % U)
                    if u in (0, 2) and not (isinstance(q, int) and q == 0):
                        (route_add if u == 0 else route_ranks)(q - 1)
                    dve.wait_ge(pT_ps, b * NG + 1)
                    dve.tensor_copy(pT[:, 0, :, :], ps[:, PT, :].rearrange("p (i n) -> p i n", i=GH)
                                    ).then_inc(pT_dve, 1)
                    if more1:
                        split_qk(b + 1)
                    if more2:
                        normalise(b + 2)
                    if not (isinstance(q, int) and q == 0):
                        route(q - 1, u)
                    elif u + 2 < NU:
                        ln1_stats(u + 3)
                    if more1:
                        copy_v(b + 1)
                        row_max(b + 1, 0)
                    dve.wait_ge(o_ps, b + 1)
                    o_v = ps[:, PT, :].rearrange("p (h w) -> p h w", w=VW)
                    did(dve.reciprocal(inv_sum[:], o_v[:, :, HD:HD + 1].rearrange("p h o -> p (h o)")))
                    settle()
                    did(dve.tensor_tensor(att[:].rearrange("p (h n) -> p h n", h=HEADS), o_v[:, :, 0:HD],
                                          inv_sum[:].unsqueeze(2).to_broadcast([P, HEADS, HD]), ALU.mult))
                    settle()
                    if not (isinstance(q, int) and q == 0 and u == 0):
                        dve.wait_ge(x1_out, b * 16)
                    dve.tensor_tensor(x1[:], att[:], x_all[:, bass.ds(b, 1), :].rearrange("p o d -> p (o d)"),
                                      ALU.add).then_inc(x1_s, 1)
                    dve.wait_ge(x1_s, b + 1)
                    did(dve.bn_stats(stats2[:], x1[:]))
                    settle(own=True)
                    did(dve.bn_aggr(mv2[:], stats2[:]))
                    settle()
                    dve.tensor_scalar(vare2[:], mv2[:, 1:2], 1e-5, None, ALU.add).then_inc(var2_s, 1)
                    if more1:
                        row_max(b + 1, 1)
                    if last and u == U - 1:
                        route_add(q)
                    dve.wait_ge(rstd2_s, b + 1)
                    if not (isinstance(q, int) and q == 0 and u == 0):
                        dve.wait_ge(xn2_out, b * 16)
                    dve.tensor_scalar(xn2[:], x1[:], mv2[:, 0:1], rstd2[:], ALU.subtract, ALU.mult).then_inc(xn2_s, 1)
                    if more2:
                        copy_qk(b + 2)
                    if more1:
                        row_max(b + 1, 2)
                        row_max(b + 1, 3)

            def read_logits(b, u):
                dve.wait_ge(lg_ps, b + 1)
                dve.tensor_tensor(lg[:, u, :], ps[:, PT + 1, LG + u * NE:LG + (u + 1) * NE], bg_bc[:], ALU.add
                                  ).then_inc(lg_read, 1)

            def bc(ap):
                return ap.unsqueeze(2).to_broadcast([P, U, NE])

            def experts(ap):
                return ap.rearrange("p k u -> p (k u)").unsqueeze(2).to_broadcast([P, TOPK * U, NE])

            def flat(ap):
                return ap.rearrange("p k u e -> p (k u) e")

            def route(q, u):
                if u == 0:
                    route_shift(q)
                    first_of_equals(0)
                    route_mask()
                    first_of_equals(1)
                elif u == 1:
                    route_pick(q)
                    route_terms(q)
                    route_sums()
                    route_inverse()
                elif u == 2:
                    route_places()
                    route_split()
                    route_columns()
                    route_weights(q)
                else:
                    one_hots(q)

            def route_shift(q):
                dve.wait_ge(lg_read, (q + 1) * U)
                largest(0, lg)
                dve.tensor_tensor(lgs[:], lg[:], bc(biggest[:, 0, :]), ALU.subtract).then_inc(lg_s, 1)
                did(dve.tensor_tensor(eq[:], lg[:], bc(biggest[:, 0, :]), ALU.is_equal))

            def route_mask():
                did(dve.scalar_tensor_tensor(lgm[:], onehot[:, 0], -1e30, lg[:], ALU.mult, ALU.add))
                settle()
                largest(1, lgm)
                did(dve.tensor_tensor(eq[:], lgm[:], bc(biggest[:, 1, :]), ALU.is_equal))

            def route_pick(q):
                dve.wait_ge(rank_ps, q + 1)
                did(dve.tensor_copy(run[:], picks[:]))
                did(dve.tensor_tensor(picked[:], onehot[:, 0], onehot[:, 1], ALU.add))
                settle()
                did(dve.tensor_tensor(pick_sums[:, 0], picked[:, 0], picked[:, 1], ALU.add))
                dve.tensor_tensor(pick_sums[:, 1], picked[:, 2], picked[:, 3], ALU.add).then_inc(pick_s, 1)
                dve.wait_ge(pick_s, q + 1)

            def route_terms(q):
                dve.wait_ge(ex_s, q + 1)
                did(dve.tensor_reduce(ex_sum[:], ex[:], AX_X, ALU.add))
                for k in range(TOPK):
                    did(dve.tensor_tensor(oht[:, k], onehot[:, k], ex[:], ALU.mult))
                settle()

            def route_sums():
                did(dve.tensor_reduce(top[:], oht[:], AX_X, ALU.add))
                did(dve.tensor_tensor(pick_sums[:, 0], pick_sums[:, 0], pick_sums[:, 1], ALU.add))
                settle()
                did(dve.tensor_tensor(picks[:], run[:], pick_sums[:, 0], ALU.add))
                did(dve.tensor_tensor(den[:], top[:, 0, :], top[:, 1, :], ALU.add))
                settle()

            def route_inverse():
                did(dve.scalar_tensor_tensor(den[:], ex_sum[:], 1e-8, den[:], ALU.mult, ALU.add))
                settle()
                did(dve.reciprocal(inv_den[:], den[:]))
                settle()

            def route_ranks(q):
                dve.wait_ge(rank_ps, q + 2)
                rk = ps[:, PT + 1, RK:RK + U * NE].rearrange("p (u e) -> p u e", u=U)
                for k in range(TOPK):
                    m = dve.tensor_tensor(ohr[:, k], onehot[:, k], rk, ALU.mult)
                m.then_inc(rank_read, 1)
                dve.wait_ge(rank_read, q + 1)

            def route_weights(q):
                did(dve.tensor_tensor(wtop[:], top[:], inv_den[:].unsqueeze(1).to_broadcast([P, TOPK, U]), ALU.mult))
                settle()
                did(dve.tensor_tensor(flat(ohw[:]), flat(onehot[:]), experts(wtop[:]), ALU.mult))
                settle()
                dve.wait_ge(cw_out, (q + 1) * 16)
                dve.tensor_tensor(cw[:], ohw[:, 0], ohw[:, 1], ALU.add).then_inc(cw_s, 1)

            def route_places():
                did(dve.tensor_reduce(rank[:], ohr[:], AX_X, ALU.add))
                settle()
                did(dve.tensor_copy(rank_i[:], rank[:]))
                settle()

            def route_split():
                did(dve.tensor_scalar(tile_i[:], rank_i[:], 7, None, ALU.arith_shift_right))
                did(dve.tensor_scalar(slot_i[:], rank_i[:], P - 1, None, ALU.bitwise_and))
                settle()

            def route_columns():
                did(dve.tensor_copy(slot_f[:], slot_i[:]))
                did(dve.scalar_tensor_tensor(col_f[:], code[:], -float(TPE), tile_i[:], ALU.mult, ALU.add))
                settle()

            def largest(k, values):
                did(dve.tensor_reduce(biggest[:, k, :], values[:], AX_X, ALU.max))
                settle()

            def first_of_equals(k):
                settle()
                did(dve.tensor_tensor(eq[:], eq[:], codes[:], ALU.mult))
                settle()
                did(dve.tensor_reduce(code[:, k, :], eq[:], AX_X, ALU.max))
                settle()
                did(dve.tensor_tensor(onehot[:, k], codes[:], bc(code[:, k, :]), ALU.is_equal))
                settle()

            def one_hots(q):
                for k in range(TOPK):
                    for u in range(U):
                        dve.tensor_scalar(hot_s[:, k * U + u, :], iota_s[:], slot_f[:, k, u:u + 1], None, ALU.is_equal)
                        m = dve.tensor_scalar(hot_c[:, k * U + u, :], iota_c[:], col_f[:, k, u:u + 1],
                                              tok1[:, bass.ds(q * U + u, 1)], ALU.is_equal, ALU.mult)
                m.then_inc(hot_done, 1)

            def route_add(q):
                dve.wait_ge(ids_ps, q + 1)
                if not (isinstance(q, int) and q == 0):
                    dve.wait_ge(ids_s, q)
                dve.tensor_tensor(ids[:], ids[:], ps[:, PT + 1, IDS:512], ALU.add).then_inc(ids_s, 1)

            dve.memset(act_table[:], 0.0).then_inc(table_s, 1)
            did(dve.memset(v_ext[:], 0.0))
            dve.memset(picks[:], 0.0).then_inc(rank_ps, 1)
            did(dve.memset(ids[:], 0.0))
            did(dve.memset(hot_s[:], 0.0))
            dve.memset(hot_c[:], 0.0).then_inc(hot_done, 1)
            dve.memset(cw[:], 0.0).then_inc(cw_out, 16)
            dve.memset(cw_next[:], 0.0).then_inc(xt_sb, 1)
            dve.memset(cw_now[:], 0.0).then_inc(y_s, 2)
            dve.memset(h_chunk[:, 0, 0:1], 0.0).then_inc(h_sb, 2)
            settle()
            did(dve.memset(v_ext[:, :, HD:HD + 1], 1.0))
            dve.wait_ge(x_in[0], 16)
            ln1_stats(0)
            dve.wait_ge(bias_ps, 1)
            did(dve.tensor_copy(bias_cols[:], ps[:, PT, 0:NBR]))
            dve.wait_ge(consts, 1)
            settle()
            normalise(0)
            dve.wait_ge(x_in[1], 16)
            ln1_stats(1)
            normalise(1)
            copy_qk(0)
            split_qk(0)
            dve.wait_ge(qk_lo_s, 1)
            for c in range(1, DC):
                for part, k in ((kmask_hi, qk_hi), (kmask_lo, qk_lo)):
                    m = dve.tensor_tensor(part[:, c, :, :],
                                          k[:, DC + c:DC + c + 1, :].bitcast(F32).to_broadcast([P, HC, P]),
                                          head_mask[:].unsqueeze(2).to_broadcast([P, HC, P]), ALU.mult)
                m.then_inc(kmask_first_s, 1)
            dve.wait_ge(bcast_in, 32)
            copy_v(0)
            dve.wait_ge(x_in[2], 16)
            ln1_stats(2)
            for g in range(NG):
                row_max(0, g)
            copy_qk(1)
            first_steps = step[0]
            counts = []

            def counted(q, last):
                body(q, last)
                counts.append(step[0])
            groups(dve, counted)
            assert counts[0] == FIRST_GROUP and counts[1] == PER_GROUP, counts
            last = NU - 1
            read_logits(NB - 1, U - 1)
            route_shift(last)
            first_of_equals(0)
            route_mask()
            first_of_equals(1)
            route_pick(last)
            route_terms(last)
            route_sums()
            dve.tensor_copy(cnt_f[:], picks[:]).then_inc(run_s, 1)
            route_ranks(last)
            did(dve.tensor_reduce(rank[:], ohr[:], AX_X, ALU.add))
            did(dve.scalar_tensor_tensor(den[:], ex_sum[:], 1e-8, den[:], ALU.mult, ALU.add))
            settle()
            did(dve.tensor_copy(rank_i[:], rank[:]))
            did(dve.reciprocal(inv_den[:], den[:]))
            settle()
            did(dve.tensor_scalar(tile_i[:], rank_i[:], 7, None, ALU.arith_shift_right))
            did(dve.tensor_scalar(slot_i[:], rank_i[:], P - 1, None, ALU.bitwise_and))
            route_weights(last)
            route_columns()
            one_hots(last)

            dve.wait_ge(cnt_ps, 1)
            did(dve.tensor_scalar(cnt_f[:], ps[:, PT, 0:NE], float(P - 1), None, ALU.add))
            settle()
            did(dve.tensor_copy(cnt_i[:], cnt_f[:]))
            settle()
            did(dve.tensor_scalar(tiles_of[:], cnt_i[:], P.bit_length() - 1, None, ALU.arith_shift_right))
            settle()
            did(dve.tensor_scalar(tiles_f[:], tiles_of[:], 1.0, None, ALU.add))
            settle()
            did(dve.tensor_copy(cnt_i[:], tiles_f[:]))
            settle()
            did(dve.tensor_scalar(cnt_i[:], cnt_i[:], 1, None, ALU.arith_shift_right))
            settle()
            did(dve.tensor_scalar(items[:], cnt_i[:], 2.0, None, ALU.max))
            did(dve.tensor_scalar(more_items[:], cnt_i[:], 2.0, -1.0, ALU.max, ALU.add))
            settle()
            did(dve.scalar_tensor_tensor(last_full[:], items[:], 2.0, tiles_of[:], ALU.mult, ALU.is_equal))
            settle()
            did(dve.scalar_tensor_tensor(pe_plan[:], more_items[:], 2.0, last_full[:], ALU.mult, ALU.add))
            route_add(NU)
            dve.wait_ge(ids_s, NU + 1)
            dve.tensor_scalar(ids_get[:], ids[:], -1.0, 0.0, ALU.add, ALU.max).then_inc(gets_listed, 1)
            did(dve.tensor_scalar(ids_f[:], ids[:], 0.0, float(SKIP), ALU.is_equal, ALU.mult))
            dve.wait_ge(gets_listed, 1)
            settle()
            dve.scalar_tensor_tensor(ids_put[:], ids[:], -1.0, ids_f[:], ALU.add, ALU.add).then_inc(lists, 1)

            g = dve.alloc_register("dve_item")
            dve.reg_mov(g, 1)
            pairs = dve.alloc_register("dve_pairs")
            dve.reg_mov(pairs, 0)

            def take_item(k):
                dve.wait_ge(xt_ps, k)
                turned = ps[:, OB, :].rearrange("p (c n) -> p c n", c=DC)
                dve.tensor_copy(xT_hi[:], turned).then_inc(xt_hi, 1)
                for half in range(2):
                    dve.tensor_copy(cw_next[:, half, :], rows[half][:, D:ROW])
                dve.wait_ge(xt_hi, k)
                dve.tensor_tensor(xT_lo[:], turned, xT_hi[:].bitcast(F32), ALU.subtract).then_inc(xt_sb, 1)

            dve.wait_ge(lists, 1)
            take_item(1)
            def item(e):
                k = dve.snap(g)
                hp = dve.snap(pairs)
                dve.wait_ge(xt_sb, k + 1)
                dve.wait_ge(y_s, k + 1)
                dve.tensor_copy(cw_now[:], cw_next[:]).then_inc(cw_moved, 1)
                for j in range(FC // 2):
                    two = slice(j * 2, j * 2 + 2)
                    raw = h_chunk[:, j % 2 * 2:j % 2 * 2 + 2, :]
                    dve.wait_ge(h_act, (hp + j) * 2 + 2)
                    dve.tensor_copy(hT_hi[:, two, :], raw).then_inc(h_hi, 1)
                    dve.wait_ge(h_hi, hp + j + 1)
                    dve.tensor_tensor(hT_lo[:, two, :], raw, hT_hi[:, two, :].bitcast(F32), ALU.subtract
                                      ).then_inc(h_sb, 1)
                dve.wait_ge(cw_moved, k)
                take_item(k + 1)
                dve.wait_ge(y_ps, k)
                for half in range(2):
                    m = dve.tensor_tensor(yb[:, half, :], ps[:, PT + half, 0:D],
                                          b2_bc[:, bass.ds(e, 1), :].rearrange("p o d -> p (o d)"), ALU.add)
                m.then_inc(y_b, 1)
                dve.wait_ge(y_b, k)
                dve.wait_ge(put_s, (k + 2) * 32)
                for half in range(2):
                    m = dve.tensor_scalar(yw[half][:], yb[:, half, :],
                                          cw_now[:, half, bass.ds(e, 1)], None, ALU.mult)
                m.then_inc(y_s, 1)
                dve.reg_add(g, g, 1)
                dve.reg_add(pairs, pairs, FC // 2)

            def take_bias(e, par):
                dve.tensor_copy(bias_now[par][:], bias_cols[:, bass.ds(e * FC, FC)]).then_inc(bias_s, 1)

            def expert(e, par, first=False, last=False):
                n = dve.value_load(items[0:1, bass.ds(e, 1)], min_val=2, max_val=N // ITEM)
                if not last:
                    take_bias(e + 1, 1 - par)
                if not first:
                    dve.wait_ge(hi_done, e + 1)
                    dve.tensor_tensor(w2_lo[par][:], w2_raw[par][:], w2_hi[par][:].bitcast(F32), ALU.subtract
                                      ).then_inc(lo2_done, 1)
                with dve.Fori(0, n) as _i:
                    item(e)

            take_bias(0, 0)
            dve.wait_ge(b2_in, 16)
            expert(0, 0, first=True)
            with dve.Fori(0, NE // 2 - 1) as pair:
                expert(pair * 2 + 1, 1)
                expert(pair * 2 + 2, 0)
            expert(NE - 1, 1, last=True)

        @block.gpsimd
        def _(pool):
            n = [0]

            def did(m):
                n[0] += 1
                m.then_inc(pool_step, 1)

            def settle():
                pool.wait_ge(pool_step, n[0])

            did(pool.memset(ident[:], 0.0))
            did(pool.memset(head_mask[:], SCALE))
            did(pool.memset(ones_bf[:], 1.0))
            did(pool.memset(minus_half[:], -0.5))
            did(pool.iota(iota_i[:], pattern=[[1, P]], base=0, channel_multiplier=0))
            did(pool.iota(codes_i[:], pattern=[[0, U], [-1, NE]], base=NE, channel_multiplier=0))
            did(pool.iota(tok_i[:], pattern=[[P, NB]], base=1, channel_multiplier=1))
            settle()
            did(pool.affine_select(out=ident[:], in_=ident[:], compare_op=ALU.not_equal, fill=1.0, base=0,
                                   pattern=[[-1, P]], channel_multiplier=1))
            did(pool.affine_select(out=earlier[:], in_=ones_bf[:], compare_op=ALU.is_gt, fill=0.0, base=0,
                                   pattern=[[1, P]], channel_multiplier=-1))
            did(pool.affine_select(out=head_mask[:], in_=head_mask[:], compare_op=ALU.is_ge, fill=0.0, base=0,
                                   pattern=[[-HD, HC]], channel_multiplier=1))
            did(pool.tensor_copy(iota_s[:], iota_i[:]))
            did(pool.tensor_copy(codes[:], codes_i[:]))
            did(pool.tensor_copy(tok1[:], tok_i[:]))
            settle()
            did(pool.tensor_scalar(iota_c[:], iota_s[:], -float(NE * TPE), None, ALU.add))
            did(pool.affine_select(out=head_mask[:], in_=head_mask[:], compare_op=ALU.is_ge, fill=0.0, base=HD - 1,
                                   pattern=[[HD, HC]], channel_multiplier=-1))
            settle()
            pool.memset(yw[0][:], 0.0).then_inc(consts, 1)

            def ln1_rstd(part):
                first, end = ln1_ends[part], ln1_ends[part + 1]
                pool.wait_ge(stats_done, part + 1)
                pool.tensor_tensor(rstd[:, first:end], vare[:, first:end], minus_half[:, first:end], ALU.pow
                                   ).then_inc(rstd_done, 1)

            def mask_keys(b, chunks=range(DC)):
                for c in chunks:
                    for part, k, ready in ((kmask_hi, qk_hi, qk_hi_s), (kmask_lo, qk_lo, qk_lo_s)):
                        if c == 0:
                            pool.wait_ge(ready, b + 1)
                        m = pool.tensor_tensor(part[:, c, :, :],
                                               k[:, DC + c:DC + c + 1, :].bitcast(F32).to_broadcast([P, HC, P]),
                                               head_mask[:].unsqueeze(2).to_broadcast([P, HC, P]), ALU.mult)
                    m.then_inc(kmask_s, DC // len(chunks))

            def body(q, last):
                for u in range(U):
                    b = q * U + u
                    pool.wait_ge(var2_s, b + 1)
                    pool.tensor_tensor(rstd2[:], vare2[:], minus_half[:, 0:1], ALU.pow).then_inc(rstd2_s, 1)
                    if not (last and u >= U - 2):
                        pool.wait_ge(s_ps, (b + 2) * NG)
                        mask_keys(b + 2)
                    if isinstance(q, int) and q == 0 and u + 2 < NU:
                        ln1_rstd(u + 3)

            def add_rows():
                for half in range(2):
                    pool.indirect_dma_start(out_rows, bass.IndirectOffsetOnAxis(put_idx[:, half:half + 1], 0),
                                            yw[half][:], None, bounds_check=N - 1, oob_is_err=False,
                                            compute_op=ALU.add).then_inc(put_s, 16)

            for rows_of in (put_idx, put_next, put_new):
                pool.memset(rows_of[:], SKIP).then_inc(put_q, 1)
            pool.memset(yw[1][:], 0.0).then_inc(pool_step, 1)
            ln1_rstd(0)
            ln1_rstd(1)
            mask_keys(0, [0])
            pool.wait_ge(s_ps, NG)
            ln1_rstd(2)
            mask_keys(1)
            pool.wait_ge(put_q, 3)
            pool.wait_ge(pool_step, n[0] + 1)
            pool.wait_ge(consts, 1)
            add_rows()
            groups(pool, body)

            def w1_low_part(par, e, c):
                if c == 0:
                    wait_alone(pool, hi_done, e + 1)
                m = pool.tensor_tensor(w1_lo[par][:, c, :], w1_raw[par][:, c, :], w1_hi[par][:, c, :].bitcast(F32),
                                       ALU.subtract)
                if c == DC - 1:
                    m.then_inc(lo1_done, 1)

            for c in range(DC):
                w1_low_part(0, 0, c)
            pool.tensor_tensor(w2_lo[0][:], w2_raw[0][:], w2_hi[0][:].bitcast(F32), ALU.subtract
                               ).then_inc(lo2_done, 1)
            pool.wait_ge(gets_listed, 1)
            pool.wait_ge(xn2_out, NB * 16)
            pool.wait_ge(cw_out, (NU + 1) * 16)
            pool.wait_ge(x1_out, NB * 16)
            g = pool.alloc_register("pool_item")
            pool.reg_mov(g, 1)

            def get_rows():
                for half in range(2):
                    pool.indirect_dma_start(rows[half][:], None, table,
                                            bass.IndirectOffsetOnAxis(get_idx[:, half:half + 1], 0)
                                            ).then_inc(gat, 16)

            def put_rows(k, col):
                wait_alone(pool, put_s, k * 32)
                wait_alone(pool, put_q, k * 3)
                pool.tensor_copy(put_idx[:], put_next[:]).then_inc(put_q, 1)
                wait_alone(pool, put_q, k * 3 + 1)
                pool.tensor_copy(put_next[:], put_new[:]).then_inc(put_q, 1)
                wait_alone(pool, put_q, k * 3 + 2)
                pool.tensor_copy(put_new[:], ids_put[:, bass.ds(col, 2)]).then_inc(put_q, 1)
                wait_alone(pool, y_s, k)
                add_rows()

            def next_rows(k, col):
                wait_alone(pool, xt_sb, k)
                pool.tensor_copy(get_idx[:], ids_get[:, bass.ds(col, 2)]).then_inc(idx_s, 1)
                wait_alone(pool, idx_s, k)
                get_rows()

            def item(e, i, par=None, fetched=False):
                k = pool.snap(g)
                col = e * TPE + i * 2
                if not fetched:
                    next_rows(k, col)
                if par is not None:
                    w1_low_part(par, e, 0)
                put_rows(k, col)
                if par is not None:
                    for c in range(1, DC):
                        w1_low_part(par, e, c)
                pool.reg_add(g, g, 1)

            def expert(e, par, fetched=False):
                m = pool.value_load(more_items[0:1, bass.ds(e, 1)], min_val=1, max_val=N // ITEM - 1)
                item(e, 0, par, fetched)
                with pool.Fori(0, m) as i:
                    item(e, i + 1)

            next_rows(1, 0)
            pool.wait_ge(lists, 1)
            expert(0, None, fetched=True)
            with pool.Fori(0, NE // 2 - 1) as pair:
                expert(pair * 2 + 1, 1)
                expert(pair * 2 + 2, 0)
            expert(NE - 1, 1)
            k = pool.snap(g)
            wait_alone(pool, xt_sb, k)
            get_rows()
            put_rows(k, 0)
            put_rows(k + 1, 0)
            wait_alone(pool, gat, k * 32)


_INS = ["x", "ctx_1024", "L0_xattn_wq", "L0_xattn_bq", "L0_xattn_wk", "L0_xattn_bk", "L0_xattn_wv", "L0_xattn_bv",
        "L0_ffn_Wg", "L0_ffn_bg", "L0_ffn_W1", "L0_ffn_b1", "L0_ffn_W2", "L0_ffn_b2"]


def kernel(**inputs):
    import numpy as _np
    import concourse.bacc as _bacc
    from concourse import mybir as _mybir
    from concourse.bass_utils import run_bass_kernel_spmd as _run

    nc = _bacc.Bacc("TRN2", target_bir_lowering=False, num_devices=1)
    arrays, args = {}, []
    for name in _INS:
        a = _np.ascontiguousarray(inputs[name])
        arrays[f"in_{name}"] = a
        args.append(nc.dram_tensor(f"in_{name}", a.shape, _mybir.dt.from_np(a.dtype), kind="ExternalInput").ap())
    shape = arrays["in_x"].shape
    args.append(nc.dram_tensor("out_0", shape, _mybir.dt.float32, kind="ExternalOutput").ap())
    build_xattn_moe(nc, *args)
    r = _run(nc, [arrays], core_ids=[0])
    return r.results[0]["out_0"]
```
